# Optimizing a Trainium2 kernel written in Bass

```python
import numpy as np
import jax
import jax.numpy as jnp

def _softmax(x, axis=-1):
    return jax.nn.softmax(x, axis=axis)

def _gelu(x):
    return jax.nn.gelu(x, approximate=True)

def _silu(x):
    return jax.nn.silu(x)

def _sigmoid(x):
    return jax.nn.sigmoid(x)

def _layernorm(x, axis=-1, eps=1e-05):
    m = jnp.mean(x, axis=axis, keepdims=True)
    v = jnp.var(x, axis=axis, keepdims=True)
    return (x - m) / jnp.sqrt(v + eps)

def _scatter_add(tgt, idx, src, axis=0):
    return tgt.at[idx].add(src)

def _segment_sum(src, seg, n):
    return jax.ops.segment_sum(src, seg, n)
kernel_name = 'mk_decoder_postln_d1_seqx_r4_ea8e71'

def setup_inputs(seed: int=0):
    np.random.seed(seed)
    _w = jnp.asarray

    def _rec_inputs():
        import jax
        import jax.numpy as jnp
        _rk = jax.random.key(seed)
        x = 7.22e-05 + 1 * jax.random.normal(jax.random.fold_in(_rk, 1), (32, 256, 256), jnp.float32)
        _lenS = 256 - jax.random.randint(jax.random.fold_in(_rk, 7), (32,), 0, max(1, 256 // 4) + 1, jnp.int32)
        _lenS2 = 256 - jax.random.randint(jax.random.fold_in(_rk, 8), (32,), 0, max(1, 256 // 4) + 1, jnp.int32)
        _ctx_1024P = jax.random.normal(jax.random.fold_in(_rk, 11), (32, 16, 256), jnp.float32)
        _ctx_1024c = jax.random.dirichlet(jax.random.fold_in(_rk, 511), 0.3 * jnp.ones((16,), jnp.float32), (32, 256))
        _ctx_1024t = jnp.einsum('bsk,bkd->bsd', _ctx_1024c, _ctx_1024P)
        _ctx_1024t = _ctx_1024t * jax.lax.rsqrt(jnp.mean(jnp.square(_ctx_1024t)) + 1e-12) * 0.953939
        ctx_1024 = 4.13588e-05 + 0.999923 * (_ctx_1024t + 0.3 * jax.random.normal(jax.random.fold_in(_rk, 611), (32, 256, 256), jnp.float32))
        _validS = jnp.arange(256)[None, :] < _lenS[:, None]
        _validS2 = jnp.arange(256)[None, :] < _lenS2[:, None]
        _causal = jnp.tril(jnp.ones((256, 256), dtype=bool))
        mask_Bx1x1xS2_ik0 = jnp.where(jnp.broadcast_to(_validS2[:, None, None, :], (32, 1, 1, 256)), 0, 1).astype(jnp.int32)
        return (x, ctx_1024, mask_Bx1x1xS2_ik0)
    x, ctx_1024, mask_Bx1x1xS2_ik0 = _rec_inputs()

    def _L0_attn_setup():
        import jax, jax.numpy as jnp
        import numpy as np
        HIDDEN = 256
        N_HEAD = 16
        HEAD_DIM = HIDDEN // N_HEAD
        BATCH = 1
        SEQ = 1024
        THETA = 10000.0

        def _rope_cos_sin(seq_len, head_dim, dtype=jnp.float32):
            inv_freq = 1.0 / THETA ** (jnp.arange(0, head_dim, 2, dtype=dtype) / head_dim)
            t = jnp.arange(seq_len, dtype=dtype)
            freqs = jnp.outer(t, inv_freq)
            return (jnp.cos(freqs), jnp.sin(freqs))

        def _apply_rope(x, cos, sin):
            x2 = x.reshape(*x.shape[:-1], -1, 2)
            x_re, x_im = (x2[..., 0], x2[..., 1])
            c = cos[None, :, None, :]
            s = sin[None, :, None, :]
            out_re = x_re * c - x_im * s
            out_im = x_re * s + x_im * c
            out = jnp.stack([out_re, out_im], axis=-1)
            return out.reshape(x.shape)
        key = jax.random.key(seed)
        kx, kq, kk, kv = jax.random.split(key, 4)
        scale = 1.0 / np.sqrt(HIDDEN)
        return {'x': jax.random.normal(kx, (BATCH, SEQ, HIDDEN), dtype=jnp.float32), 'wq': jax.random.normal(kq, (HIDDEN, HIDDEN), dtype=jnp.float32) * scale, 'wk': jax.random.normal(kk, (HIDDEN, HIDDEN), dtype=jnp.float32) * scale, 'wv': jax.random.normal(kv, (HIDDEN, HIDDEN), dtype=jnp.float32) * scale}
    _L0_attn_all = _L0_attn_setup()
    _L0_attn_in = {k: v for k, v in _L0_attn_all.items() if k in ('wq', 'wk', 'wv')}
    del _L0_attn_all

    def _L0_xattn_setup():
        import jax, jax.numpy as jnp
        import numpy as np
        BS, SEQ, D_MODEL, N_HEADS = (4, 512, 256, 16)
        D_HEAD = D_MODEL // N_HEADS

        def _split_heads(x):
            b, s, _ = x.shape
            return x.reshape(b, s, N_HEADS, D_HEAD).transpose(0, 2, 1, 3)
        key = jax.random.key(seed)
        ks = jax.random.split(key, 12)
        s = 1.0 / np.sqrt(D_MODEL)
        return {'Q': jax.random.normal(ks[0], (BS, SEQ, D_MODEL), jnp.float32), 'K': jax.random.normal(ks[1], (BS, SEQ, D_MODEL), jnp.float32), 'V': jax.random.normal(ks[2], (BS, SEQ, D_MODEL), jnp.float32), 'mask': jax.random.randint(ks[3], (BS, 1, 1, SEQ), 0, 2, jnp.int32), 'Wq': jax.random.normal(ks[4], (D_MODEL, D_MODEL), jnp.float32) * s, 'bq': jnp.zeros((D_MODEL,), jnp.float32), 'Wk': jax.random.normal(ks[5], (D_MODEL, D_MODEL), jnp.float32) * s, 'bk': jnp.zeros((D_MODEL,), jnp.float32), 'Wv': jax.random.normal(ks[6], (D_MODEL, D_MODEL), jnp.float32) * s, 'bv': jnp.zeros((D_MODEL,), jnp.float32), 'Wo': jax.random.normal(ks[7], (D_MODEL, D_MODEL), jnp.float32) * s, 'bo': jnp.zeros((D_MODEL,), jnp.float32)}
    _L0_xattn_all = _L0_xattn_setup()
    _L0_xattn_in = {k: v for k, v in _L0_xattn_all.items() if k in ('Wq', 'bq', 'Wk', 'bk', 'Wv', 'bv', 'Wo', 'bo')}
    del _L0_xattn_all

    def _L0_ffn_setup():
        import math
        import jax, jax.numpy as jnp
        import numpy as np
        D_MODEL = 256
        D_HIDDEN = 1024
        N_EXPERTS = 8
        TOP_K = 2
        CAPACITY_FACTOR = 1.25
        key = jax.random.key(seed)
        ks = jax.random.split(key, 8)
        s = 0.02
        x = jax.random.normal(ks[0], (4, 512, D_MODEL), dtype=jnp.float32)
        router_w = jax.random.normal(ks[1], (D_MODEL, N_EXPERTS), dtype=jnp.float32) * s
        router_b = jnp.zeros((N_EXPERTS,), dtype=jnp.float32)
        w1 = jax.random.normal(ks[2], (N_EXPERTS, D_MODEL, D_HIDDEN), dtype=jnp.float32) * s
        b1 = jnp.zeros((N_EXPERTS, D_HIDDEN), dtype=jnp.float32)
        w2 = jax.random.normal(ks[3], (N_EXPERTS, D_HIDDEN, D_MODEL), dtype=jnp.float32) * s
        b2 = jnp.zeros((N_EXPERTS, D_MODEL), dtype=jnp.float32)
        return {'x': x, 'router_w': router_w, 'router_b': router_b, 'w1': w1, 'b1': b1, 'w2': w2, 'b2': b2}
    _L0_ffn_all = _L0_ffn_setup()
    _L0_ffn_in = {k: v for k, v in _L0_ffn_all.items() if k in ('router_w', 'router_b', 'w1', 'b1', 'w2', 'b2')}
    del _L0_ffn_all
    return {'x': x, 'ctx_1024': ctx_1024, 'mask_Bx1x1xS2_ik0': mask_Bx1x1xS2_ik0, 'L0_attn_wq': _L0_attn_in['wq'], 'L0_attn_wk': _L0_attn_in['wk'], 'L0_attn_wv': _L0_attn_in['wv'], 'L0_xattn_Wq': _L0_xattn_in['Wq'], 'L0_xattn_bq': _L0_xattn_in['bq'], 'L0_xattn_Wk': _L0_xattn_in['Wk'], 'L0_xattn_bk': _L0_xattn_in['bk'], 'L0_xattn_Wv': _L0_xattn_in['Wv'], 'L0_xattn_bv': _L0_xattn_in['bv'], 'L0_xattn_Wo': _L0_xattn_in['Wo'], 'L0_xattn_bo': _L0_xattn_in['bo'], 'L0_ffn_router_w': _L0_ffn_in['router_w'], 'L0_ffn_router_b': _L0_ffn_in['router_b'], 'L0_ffn_w1': _L0_ffn_in['w1'], 'L0_ffn_b1': _L0_ffn_in['b1'], 'L0_ffn_w2': _L0_ffn_in['w2'], 'L0_ffn_b2': _L0_ffn_in['b2']}

def reference(x, ctx_1024, mask_Bx1x1xS2_ik0, L0_attn_wq, L0_attn_wk, L0_attn_wv, L0_xattn_Wq, L0_xattn_bq, L0_xattn_Wk, L0_xattn_bk, L0_xattn_Wv, L0_xattn_bv, L0_xattn_Wo, L0_xattn_bo, L0_ffn_router_w, L0_ffn_router_b, L0_ffn_w1, L0_ffn_b1, L0_ffn_w2, L0_ffn_b2):
    import jax
    import jax.numpy as jnp

    def _L0_attn_ref(x, wq, wk, wv):
        import jax, jax.numpy as jnp
        import numpy as np
        HIDDEN = 256
        N_HEAD = 16
        HEAD_DIM = HIDDEN // N_HEAD
        BATCH = 1
        SEQ = 1024
        THETA = 10000.0

        def _rope_cos_sin(seq_len, head_dim, dtype=jnp.float32):
            inv_freq = 1.0 / THETA ** (jnp.arange(0, head_dim, 2, dtype=dtype) / head_dim)
            t = jnp.arange(seq_len, dtype=dtype)
            freqs = jnp.outer(t, inv_freq)
            return (jnp.cos(freqs), jnp.sin(freqs))

        def _apply_rope(x, cos, sin):
            x2 = x.reshape(*x.shape[:-1], -1, 2)
            x_re, x_im = (x2[..., 0], x2[..., 1])
            c = cos[None, :, None, :]
            s = sin[None, :, None, :]
            out_re = x_re * c - x_im * s
            out_im = x_re * s + x_im * c
            out = jnp.stack([out_re, out_im], axis=-1)
            return out.reshape(x.shape)
        B, S, _ = x.shape
        xq = (x @ wq.T).reshape(B, S, N_HEAD, HEAD_DIM).astype(jnp.float32)
        xk = (x @ wk.T).reshape(B, S, N_HEAD, HEAD_DIM).astype(jnp.float32)
        xv = (x @ wv.T).reshape(B, S, N_HEAD, HEAD_DIM).astype(jnp.float32)
        cos, sin = _rope_cos_sin(S, HEAD_DIM)
        q = _apply_rope(xq, cos, sin)
        k = _apply_rope(xk, cos, sin)
        scores = jnp.einsum('bqhd,bkhd->bhqk', q, k) / jnp.sqrt(jnp.asarray(HEAD_DIM, dtype=q.dtype))
        attn = jax.nn.softmax(scores, axis=-1)
        out = jnp.einsum('bhqk,bkhd->bqhd', attn, xv)
        return out.reshape(B, S, N_HEAD * HEAD_DIM)

    def _L0_xattn_ref(Q, K, V, mask, Wq, bq, Wk, bk, Wv, bv, Wo, bo):
        import jax, jax.numpy as jnp
        import numpy as np
        BS, SEQ, D_MODEL, N_HEADS = (4, 512, 256, 16)
        D_HEAD = D_MODEL // N_HEADS

        def _split_heads(x):
            b, s, _ = x.shape
            return x.reshape(b, s, N_HEADS, D_HEAD).transpose(0, 2, 1, 3)
        q = _split_heads(Q @ Wq.T + bq)
        k = _split_heads(K @ Wk.T + bk)
        v = _split_heads(V @ Wv.T + bv)
        scores = jnp.einsum('bhqd,bhkd->bhqk', q, k) / np.sqrt(D_HEAD).astype(np.float32)
        scores = jnp.where(mask == 0, jnp.float32(-1000000000.0), scores)
        attn = jax.nn.softmax(scores, axis=-1)
        ctx = jnp.einsum('bhqk,bhkd->bhqd', attn, v)
        b, h, s, d = ctx.shape
        ctx = ctx.transpose(0, 2, 1, 3).reshape(b, s, h * d)
        return ctx @ Wo.T + bo

    def _L0_ffn_ref(x, router_w, router_b, w1, b1, w2, b2):
        import math
        import jax, jax.numpy as jnp
        import numpy as np
        D_MODEL = 256
        D_HIDDEN = 1024
        N_EXPERTS = 8
        TOP_K = 2
        CAPACITY_FACTOR = 1.25
        B, T, D = x.shape
        N = B * T
        E = N_EXPERTS
        capacity = max(1, math.ceil(N / E * CAPACITY_FACTOR))
        x_flat = x.reshape(N, D)
        logits = x_flat.astype(jnp.float32) @ router_w + router_b
        gates = jax.nn.softmax(logits, axis=-1)
        _, topk_idx = jax.lax.top_k(gates, TOP_K)
        expert_mask = jax.nn.one_hot(topk_idx, E, dtype=jnp.int32).sum(1)
        pos = jnp.cumsum(expert_mask, axis=0) - 1
        expert_mask = expert_mask * (pos < capacity)
        valid = expert_mask > 0
        pos_c = jnp.where(valid, pos, capacity)
        e_idx = jnp.broadcast_to(jnp.arange(E), (N, E))
        dispatched = x_flat[:, None, :] * valid[:, :, None].astype(x.dtype)
        buf = jnp.zeros((E, capacity + 1, D), x.dtype).at[e_idx.ravel(), pos_c.ravel()].add(dispatched.reshape(N * E, D))
        buf = buf[:, :capacity]
        h = jax.nn.gelu(jnp.einsum('ecd,edh->ech', buf, w1) + b1[:, None, :], approximate=False)
        out = jnp.einsum('ech,ehd->ecd', h, w2) + b2[:, None, :]
        pos_g = jnp.minimum(pos_c, capacity - 1)
        gathered = out[e_idx, pos_g]
        weights = (gates * valid).astype(x.dtype)
        y = jnp.einsum('ned,ne->nd', gathered, weights)
        return y.reshape(B, T, D)
    x = _layernorm(x + _L0_attn_ref(x, L0_attn_wq, L0_attn_wk, L0_attn_wv), axis=-1)
    x = _layernorm(x + _L0_xattn_ref(x, ctx_1024, ctx_1024, mask_Bx1x1xS2_ik0, L0_xattn_Wq, L0_xattn_bq, L0_xattn_Wk, L0_xattn_bk, L0_xattn_Wv, L0_xattn_bv, L0_xattn_Wo, L0_xattn_bo), axis=-1)
    x = _layernorm(x + _L0_ffn_ref(x, L0_ffn_router_w, L0_ffn_router_b, L0_ffn_w1, L0_ffn_b1, L0_ffn_w2, L0_ffn_b2), axis=-1)
    return x

_drawn_inputs = setup_inputs


def setup_inputs(seed=0):
    import zlib

    import numpy as np

    out = dict(_drawn_inputs(seed))
    spreads = {'L0_xattn_bq': (0.0, 0.32),
     'L0_xattn_bk': (0.0, 0.8),
     'L0_xattn_bv': (0.0, 0.1),
     'L0_xattn_bo': (0.0, 0.1),
     'L0_ffn_router_b': (0.0, 0.455),
     'L0_ffn_b1': (0.0, 0.8),
     'L0_ffn_b2': (0.0, 0.397)}
    factors = {}
    for name, (base, spread) in spreads.items():
        noise = np.random.default_rng([zlib.crc32(name.encode()), seed]).standard_normal(out[name].shape)
        drawn = base * np.exp(spread * noise) if base else spread * noise
        out[name] = jnp.asarray(drawn.astype(out[name].dtype))
    for name, factor in factors.items():
        out[name] = (out[name] * factor).astype(out[name].dtype)
    return out
```

```python
from contextlib import ExitStack

import numpy as np

import concourse.bass as bass
from concourse import mybir

F32 = mybir.dt.float32
BF16 = mybir.dt.bfloat16
U32 = mybir.dt.uint32
I32 = mybir.dt.int32
ALU = mybir.AluOpType
ACT = mybir.ActivationFunctionType
AX = mybir.AxisListType

P = 128
D = 256
H = 16
R = D // H
S = 256
T2 = S // P
KD = D // P
SLOTS = 6
DATA = SLOTS * R
MASKED = DATA + 3
STACK = MASKED + 3
SCALE = 1.0 / 4.0
MASK_VALUE = -1.0e9 / SCALE
EPS = 1e-5
SELF, CROSS = 0, 1
Q, K = 0, 1
PART_SLOTS = {Q: [(0, 2, 4), (1, 3), (5,)], K: [(0, 3, 5), (1, 2), (4,)]}


def bf16_parts(value):
    parts, rest = [], np.float32(value)
    for _ in range(3):
        part = (np.float32(rest).reshape(1).view(np.uint32) & np.uint32(0xFFFF0000)).view(np.float32)[0]
        parts.append(float(part))
        rest = np.float32(rest - part)
    assert rest == 0
    return parts


class Steps:

    def __init__(self, sem, per):
        self.sem, self.per = sem, per

    def count(self, b, k=None):
        return b * self.per + (self.per if k is None else k)

    def due(self, b, k=None):
        value = self.count(b, k)
        return not isinstance(value, int) or value > 0


class Tally:

    def __init__(self):
        self.n = 0

    def one(self):
        self.n += 1
        return self.n


def attention(nc, x_rows, x_cols, ctx_cols, mask_cols, w_self, w_cross, biases, tables, router, x2_out,
              slots, logits, NB):
    ctx = ExitStack()
    with ctx:
        def sb(name, shape, dt=F32):
            return ctx.enter_context(nc.sbuf_tensor(name, shape, dt))

        def steps(name, per):
            return Steps(ctx.enter_context(nc.semaphore(name)), per)

        def both(name, per_self, per_cross=None):
            return [steps(name + "_self", per_self), steps(name + "_cross", per_cross or per_self)]

        wqk = [sb(f"wqk{t}", [P, KD, 2 * D]) for t in (SELF, CROSS)]
        wv = [sb(f"wv{t}", [P, KD, D]) for t in (SELF, CROSS)]
        wo = sb("wo", [P, KD, D])
        rw = sb("rw", [P, KD, 8])
        rb = sb("rb", [P, 8])
        bias_qk = sb("bias_qk", [P, 2 * D])
        bias_v = sb("bias_v", [P, D])
        bias_o = sb("bias_o", [P, D])
        rope_c = sb("rope_c", [P, T2, R // 2])
        rope_s = sb("rope_s", [P, T2, R // 2])
        ident = sb("ident", [P, P])
        ident_b = sb("ident_b", [P, P], BF16)
        mask_i = sb("mask_i", [P, 32 * T2], I32)
        mask_f = sb("mask_f", [P, 32 * T2])
        hidden_f = sb("hidden_f", [P, 32 * T2])
        mask_all = sb("mask_all", [P, 32, T2, 4])
        mask_now = sb("mask_now", [P, T2, 4])
        src = [sb("xT", [P, KD, S]), sb("ctxT", [P, KD, S])]
        x_res = sb("x_res", [P, T2, D])
        qk = [sb(f"qk{t}", [P, T2, 2 * D]) for t in (SELF, CROSS)]
        rot = sb("rot", [P, T2, 2 * D])
        rest = sb("rest", [P, T2, 2 * D])
        rest2 = sb("rest2", [P, T2, 2 * D])
        parts = [sb(f"parts{t}", [P, T2, 2, H, STACK], BF16) for t in (SELF, CROSS)]
        stack = [sb(f"stack{t}", [P, 2, H, S], BF16) for t in (SELF, CROSS)]
        val = [sb(f"val{t}", [P, T2, H, 32]) for t in (SELF, CROSS)]
        smax = sb("smax", [P, T2, H])
        nmax = sb("nmax", [P, T2, H])
        nrest = sb("nrest", [P, T2, H])
        nrest2 = sb("nrest2", [P, T2, H])
        nparts = sb("nparts", [P, T2, 3, H], BF16)
        nrows = sb("nrows", [3 * H, S], BF16)
        prob = sb("prob", [P, 4, 2 * S])
        outT = [sb(f"outT{t}", [P, 4, S]) for t in (SELF, CROSS)]
        rden = sb("rden", [P, T2, H])
        att = sb("att", [P, T2, D])
        y = sb("y", [P, T2, D])
        stats = sb("stats", [P, T2, 6])
        mv = [sb(f"mv{t}", [P, T2, 2]) for t in (SELF, CROSS)]
        rstd = [sb(f"rstd{t}", [P, T2]) for t in (SELF, CROSS)]
        veps = [sb(f"veps{t}", [P, T2]) for t in (SELF, CROSS)]
        minus_half = sb("minus_half", [P, T2])
        x1 = sb("x1", [P, T2, D])
        x1b = sb("x1b", [P, T2, D])
        x1T = sb("x1T", [P, KD, S])
        att2 = sb("att2", [P, T2, D])
        attT = sb("attT", [P, KD, S])
        y2 = sb("y2", [P, T2, D])
        stats2 = sb("stats2", [P, T2, 6])
        x2 = sb("x2", [P, T2, D])
        x2T = sb("x2T", [P, KD, S])
        zero = sb("zero", [P, 8 * D])
        ps_s = ctx.enter_context(nc.psum_tensor("ps_s", [P, 2, T2, S], F32))
        ps_e = ctx.enter_context(nc.psum_tensor("ps_e", [P, 2, T2, S], F32))
        ps_o = ctx.enter_context(nc.psum_tensor("ps_o", [P, 512], F32))
        ps_t = ctx.enter_context(nc.psum_tensor("ps_t", [P, 2, 4, S], BF16))
        ps_p = ctx.enter_context(nc.psum_tensor("ps_p", [P, 512], F32))
        ps_pb = ps_p[:, :].bitcast(BF16)

        load_w = steps("load_w", 16 * 16)
        src_in = both("src_in", 16)
        res_in = steps("res_in", 16)
        max_in = both("max_in", 48)
        x2_sent = steps("x2_sent", 16)
        consts = steps("consts", 8)
        masks = steps("masks", 6)
        zeroed = steps("zeroed", 1)
        slots_zero = ctx.enter_context(nc.semaphore("slots_zero"))
        v_mm = both("v_mm", 1)
        v_ev = both("v_ev", 1)
        qk_mm = both("qk_mm", 2)
        qk_ev = both("qk_ev", 6, 2)
        split_p = both("split_p", 6, 9)
        split_a = both("split_a", 6)
        split_v = both("split_v", 10)
        tr_mm = both("tr_mm", 8)
        tr_evq = both("tr_evq", 4)
        tr_evk = both("tr_evk", 4)
        s_mm = both("s_mm", 16)
        s_max = both("s_max", 16)
        neg = both("neg", 6)
        neg_mm = both("neg_mm", 1)
        neg_ev = both("neg_ev", 1)
        e_mm = both("e_mm", 16)
        e_exp = both("e_exp", 16)
        pv_mm = both("pv_mm", 16)
        pv_ev = both("pv_ev", 4)
        o_mm = both("o_mm", 2)
        ln = both("ln", 12, 11)
        ln_r = both("ln_r", 2)
        col_mm = both("col_mm", 1)
        col_ev = both("col_ev", 1)
        proj_mm = steps("proj_mm", 1)
        x1b_made = steps("x1b_made", 1)
        x2T_mm = steps("x2T_mm", 1)
        x2T_ev = steps("x2T_ev", 1)
        r_mm = steps("r_mm", 1)
        r_ev = steps("r_ev", 1)
        fences = {e: ctx.enter_context(nc.semaphore("fence_" + e)) for e in ("pool", "pe", "dve")}

        def slots_of(emit, eng, loop_first=3):
            def step(i):
                emit(i, SELF, CROSS, i, i - 2)
                emit(i, CROSS, SELF, i - 1, i)
            last_full = NB - 2
            first = min(loop_first, NB + 2)
            for i in range(first):
                step(i)
            if first <= last_full:
                with eng.Fori(first, last_full + 1) as i:
                    step(i)
                first = last_full + 1
            for i in range(first, NB + 2):
                step(i)

        def there(b):
            return not isinstance(b, int) or 0 <= b < NB

        def before(T, b):
            other = b - 2 if T == SELF else b + 1
            return min(other, NB - 1) if isinstance(other, int) else other

        def by_head(a, t):
            return a[:, t, :].rearrange("p (c h r) -> p c h r", c=2, h=H)

        def put_parts(copy, Y, t, part, n, level):
            more = [x for x in PART_SLOTS[part][n] if n == 2 or x != n]
            slots = parts[Y][:, t, part, :, 0:DATA].rearrange("p h (s r) -> p h s r", r=R)
            return copy(slots[:, :, more[0]:more[-1] + 1:2, :], by_head(level, t)[:, part]
                        .unsqueeze(2).to_broadcast([P, H, len(more), R]))

        def first_step(Y):
            return 3 if Y == SELF else 6

        def stack_steps(Y):
            return (13, 15, 17, 19) if Y == SELF else (16, 17, 18, 19)

        block = ctx.enter_context(nc.Block())

        def load_src(sp, T, b):
            cols = (x_cols, ctx_cols)[T]
            if isinstance(b, int) and b == 0:
                a = cols[0:1]
            else:
                a = cols[bass.ds(b, 1)]
            sp.dma_start(src[T][:, :, :], a.rearrange("b (k p) s -> p (b k) s", p=P)).then_inc(src_in[T].sem, 16)

        def load_res(sp, b):
            a = x_rows[0:1] if isinstance(b, int) and b == 0 else x_rows[bass.ds(b, 1)]
            sp.dma_start(x_res[:, :, :], a.rearrange("b (t p) d -> p (b t) d", p=P)).then_inc(res_in.sem, 16)

        @block.sync
        def _(sp):
            loads = [
                (wqk[SELF][:, :, :], w_self["qk"].rearrange("(k p) n -> p k n", p=P)),
                (src[SELF][:, :, :], None),
                (wv[SELF][:, :, :], w_self["v"].rearrange("(k p) n -> p k n", p=P)),
                (wqk[CROSS][:, :, 0:D], w_cross["q"].rearrange("(k p) n -> p k n", p=P)),
                (wqk[CROSS][:, :, D:2 * D], w_cross["k"].rearrange("(k p) n -> p k n", p=P)),
                (wv[CROSS][:, :, :], w_cross["v"].rearrange("(k p) n -> p k n", p=P)),
                (wo[:, :, :], w_cross["o"].rearrange("(k p) n -> p k n", p=P)),
                (rope_c[:, :, :], tables["cos"].rearrange("(t p) r -> p t r", p=P)),
                (rope_s[:, :, :], tables["sin"].rearrange("(t p) r -> p t r", p=P)),
                (ident[:, :], tables["ident"]),
                (mask_i[:, :], mask_cols),
                (rw[:, :, :], router["w"].rearrange("(k p) e -> p k e", p=P)),
                (rb[:, :], router["b"].partition_broadcast(P)),
                (bias_qk[:, 0:D], biases["q"].partition_broadcast(P)),
                (bias_qk[:, D:2 * D], biases["k"].partition_broadcast(P)),
                (bias_v[:, :], biases["v"].partition_broadcast(P)),
                (bias_o[:, :], biases["o"].partition_broadcast(P)),
            ]
            n = 0
            for dst, a in loads:
                if a is None:
                    load_src(sp, SELF, 0)
                else:
                    sp.dma_start(dst, a).then_inc(load_w.sem, 16)
                    n += 16
            assert n == load_w.per, n
            load_src(sp, CROSS, 0)
            load_res(sp, 0)
            sp.wait_ge(zeroed.sem, zeroed.count(0, 1))
            for part in slots.rearrange("(n p r) d -> n p (r d)", p=P, r=8):
                sp.dma_start(part, zero[:, :]).then_inc(slots_zero, 16)

            def emit(i, X, Y, bX, bY):
                if there(bX) and there(bX + 1):
                    sp.wait_ge(v_mm[X].sem, v_mm[X].count(bX))
                    sp.wait_ge(qk_mm[X].sem, qk_mm[X].count(bX))
                    load_src(sp, X, bX + 1)
                if X == SELF and there(bX - 1) and there(bX):
                    if ln[SELF].due(bX - 1, 6):
                        sp.wait_ge(ln[SELF].sem, ln[SELF].count(bX - 1, 6))
                    load_res(sp, bX)
                if X == CROSS and there(bX - 1):
                    if ln[CROSS].due(bX - 1):
                        sp.wait_ge(ln[CROSS].sem, ln[CROSS].count(bX - 1))
                    if x2_sent.due(bX - 2):
                        sp.wait_ge(x2_sent.sem, x2_sent.count(bX - 2))
                    sp.dma_start(x2_out[bass.ds(bX - 1, 1), :, :].rearrange("b (t p) d -> p (b t) d", p=P),
                                 x2[:, :, :]).then_inc(x2_sent.sem, 16)
                if there(bX):
                    sp.wait_ge(neg_ev[X].sem, neg_ev[X].count(bX))
                    if max_in[X].due(bX - 1):
                        sp.wait_ge(max_in[X].sem, max_in[X].count(bX - 1))
                    for j in range(3):
                        sp.dma_start(stack[X][MASKED + j:MASKED + j + 1, Q, :, :],
                                     nrows[j * H:(j + 1) * H, :]).then_inc(max_in[X].sem, 16)
            slots_of(emit, sp)
            sp.wait_ge(x2_sent.sem, x2_sent.count(NB - 1))
            sp.wait_ge(slots_zero, slots.shape[0] // (8 * P) * 16)

        @block.tensor
        def _(pe):
            pe.wait_ge(load_w.sem, load_w.count(0, load_w.per))
            pe.wait_ge(consts.sem, consts.count(0))
            pe.wait_ge(masks.sem, masks.count(0))
            held = [None]

            def take_bank(reader):
                if held[0] is not None:
                    steps_of, b, k = held[0]
                    pe.wait_ge(steps_of.sem, steps_of.count(b, k))
                held[0] = reader

            def values(X, b):
                pe.wait_ge(src_in[X].sem, src_in[X].count(b))
                take_bank((v_ev[X], b, 1))
                for t in range(T2):
                    for k in range(KD):
                        mm = nc.tensor.matmul(ps_p[:, t * D:(t + 1) * D], src[X][:, k, t * P:(t + 1) * P],
                                              wv[X][:, k, :], start=(k == 0), stop=(k == KD - 1))
                mm.then_inc(v_mm[X].sem, 1)

            def project(Y, b, t):
                take_bank((qk_ev[Y], b, (t + 1) * qk_ev[Y].per // T2))
                pe.wait_ge(src_in[Y].sem, src_in[Y].count(b))
                if Y == CROSS:
                    pe.wait_ge(col_ev[SELF].sem, col_ev[SELF].count(b))
                rows = slice(t * P, (t + 1) * P)
                if Y == SELF:
                    for k in range(KD):
                        mm = nc.tensor.matmul(ps_p[:, :], src[SELF][:, k, rows], wqk[SELF][:, k, :],
                                              start=(k == 0), stop=(k == KD - 1))
                else:
                    for part, left in ((Q, x1T), (K, src[CROSS])):
                        for k in range(KD):
                            mm = nc.tensor.matmul(ps_p[:, part * D:(part + 1) * D], left[:, k, rows],
                                                  wqk[CROSS][:, k, part * D:(part + 1) * D],
                                                  start=(k == 0), stop=(k == KD - 1))
                mm.then_inc(qk_mm[Y].sem, 1)

            def make_stack(Y, b, g):
                for split in (split_p, split_a, split_v):
                    pe.wait_ge(split[Y].sem, split[Y].count(b))
                for part, ev in ((Q, tr_evq), (K, tr_evk)):
                    if g:
                        pe.wait_ge(ev[Y].sem, ev[Y].count(b, g))
                    else:
                        if ev[1 - Y].due(before(Y, b)):
                            pe.wait_ge(ev[1 - Y].sem, ev[1 - Y].count(before(Y, b)))
                        if ev[Y].due(b - 1):
                            pe.wait_ge(ev[Y].sem, ev[Y].count(b - 1))
                    for j in range(4):
                        for t in range(T2):
                            mm = nc.tensor.transpose(ps_t[0:STACK, part, j, t * P:(t + 1) * P],
                                                     parts[Y][:, t, part, 4 * g + j, :], ident_b[:, :])
                    mm.then_inc(tr_mm[Y].sem, 1)

            def scores(X, b, h):
                if h % 4 == 0:
                    pe.wait_ge(tr_evq[X].sem, tr_evq[X].count(b, h // 4 + 1))
                    pe.wait_ge(tr_evk[X].sem, tr_evk[X].count(b, h // 4 + 1))
                if h >= 2:
                    pe.wait_ge(s_max[X].sem, s_max[X].count(b, h - 1))
                elif h == 0:
                    if s_max[1 - X].due(before(X, b)):
                        pe.wait_ge(s_max[1 - X].sem, s_max[1 - X].count(before(X, b)))
                    if s_max[X].due(b - 1):
                        pe.wait_ge(s_max[X].sem, s_max[X].count(b - 1))
                for t in range(T2):
                    mm = nc.tensor.matmul(ps_s[:, h % 2, t, :], stack[X][0:MASKED, Q, h, t * P:(t + 1) * P],
                                          stack[X][0:MASKED, K, h, :], start=True, stop=True)
                mm.then_inc(s_mm[X].sem, 1)

            def shifted(Y, b, h):
                if h == 0:
                    pe.wait_ge(max_in[Y].sem, max_in[Y].count(b))
                if h >= 2:
                    pe.wait_ge(e_exp[Y].sem, e_exp[Y].count(b, h - 1))
                elif h == 0:
                    if e_exp[1 - Y].due(before(Y, b)):
                        pe.wait_ge(e_exp[1 - Y].sem, e_exp[1 - Y].count(before(Y, b)))
                    if e_exp[Y].due(b - 1):
                        pe.wait_ge(e_exp[Y].sem, e_exp[Y].count(b - 1))
                for t in range(T2):
                    mm = nc.tensor.matmul(ps_e[:, h % 2, t, :], stack[Y][0:STACK, K, h, t * P:(t + 1) * P],
                                          stack[Y][0:STACK, Q, h, :], start=True, stop=True)
                mm.then_inc(e_mm[Y].sem, 1)

            def with_values(Y, b, h):
                pe.wait_ge(e_exp[Y].sem, e_exp[Y].count(b, h + 1))
                if h == 0:
                    pe.wait_ge(v_ev[Y].sem, v_ev[Y].count(b))
                    if pv_ev[1 - Y].due(before(Y, b)):
                        pe.wait_ge(pv_ev[1 - Y].sem, pv_ev[1 - Y].count(before(Y, b)))
                    if pv_ev[Y].due(b - 1):
                        pe.wait_ge(pv_ev[Y].sem, pv_ev[Y].count(b - 1))
                elif h % 4 == 0:
                    pe.wait_ge(pv_ev[Y].sem, pv_ev[Y].count(b, h // 4))
                q = h % 4 * 32
                for t in range(T2):
                    mm = nc.tensor.matmul(ps_o[q:q + 32, 0:S], val[Y][:, t, h, :],
                                          prob[:, h % 4, t * S:(t + 1) * S], start=(t == 0), stop=(t == T2 - 1))
                mm.then_inc(pv_mm[Y].sem, 1)

            def out_rows(X, b, t):
                pe.wait_ge(pv_ev[X].sem, pv_ev[X].count(b))
                take_bank((ln[X], b, 2 + 2 * t))
                for g in range(4):
                    mm = nc.tensor.transpose(ps_p[:, g * P:(g + 1) * P], outT[X][:, g, t * P:(t + 1) * P], ident[:, :])
                mm.then_inc(o_mm[X].sem, 1)

            def columns(X, b):
                pe.wait_ge(ln[X].sem, ln[X].count(b, 12 if X == SELF else 4))
                take_bank((col_ev[X], b, 1))
                rows = x1 if X == SELF else att2
                for k in range(KD):
                    for t in range(T2):
                        mm = nc.tensor.transpose(ps_p[:, k * S + t * P:k * S + (t + 1) * P],
                                                 rows[:, t, k * P:(k + 1) * P], ident[:, :])
                mm.then_inc(col_mm[X].sem, 1)

            def project_out(b):
                pe.wait_ge(col_ev[CROSS].sem, col_ev[CROSS].count(b))
                take_bank((ln[CROSS], b, 5))
                for t in range(T2):
                    for k in range(KD):
                        mm = nc.tensor.matmul(ps_p[:, t * D:(t + 1) * D], attT[:, k, t * P:(t + 1) * P],
                                              wo[:, k, :], start=(k == 0), stop=(k == KD - 1))
                mm.then_inc(proj_mm.sem, 1)

            def x2_columns(b):
                pe.wait_ge(ln[CROSS].sem, ln[CROSS].count(b))
                take_bank((x2T_ev, b, 1))
                for k in range(KD):
                    for t in range(T2):
                        mm = nc.tensor.transpose(ps_p[:, k * S + t * P:k * S + (t + 1) * P],
                                                 x2[:, t, k * P:(k + 1) * P], ident[:, :])
                mm.then_inc(x2T_mm.sem, 1)

            def route(b):
                pe.wait_ge(x2T_ev.sem, x2T_ev.count(b))
                take_bank((r_ev, b, 1))
                for t in range(T2):
                    for k in range(KD):
                        mm = nc.tensor.matmul(ps_p[:, t * 8:(t + 1) * 8], x2T[:, k, t * P:(t + 1) * P],
                                              rw[:, k, :], start=(k == 0), stop=(k == KD - 1))
                mm.then_inc(r_mm.sem, 1)

            def max_rows(X, b):
                pe.wait_ge(neg[X].sem, neg[X].count(b))
                take_bank((neg_ev[X], b, 1))
                pe.sem_inc(fences["pe"])
                for t in range(T2):
                    mm = nc.tensor.transpose(ps_pb[0:3 * H, t * P:(t + 1) * P],
                                             nparts[:, t, :, :].rearrange("p a h -> p (a h)"), ident_b[:, :])
                mm.then_inc(neg_mm[X].sem, 1)

            def emit(i, X, Y, bX, bY):
                if X == SELF and (not isinstance(i, int) or i >= 2):
                    held[0] = (neg_ev[CROSS], i - 2, 1)
                for n in range(21):
                    if there(bX) and n < H:
                        scores(X, bX, n)
                    if there(bY) and 4 <= n < H + 4:
                        shifted(Y, bY, n - 4)
                    if there(bY) and n >= 5:
                        with_values(Y, bY, n - 5)
                    if there(bX - 1) and n < 2:
                        out_rows(X, bX - 1, n)
                    if there(bX) and n == 2:
                        values(X, bX)
                    if there(bX - 1) and n == (4 if X == SELF else 5):
                        columns(X, bX - 1)
                    if there(bX - 1) and X == CROSS:
                        if n == 7:
                            project_out(bX - 1)
                        if n == 10:
                            x2_columns(bX - 1)
                        if n == 12:
                            route(bX - 1)
                    if there(bY + 1) and n - first_step(Y) in range(T2):
                        project(Y, bY + 1, n - first_step(Y))
                    if there(bX) and n == 18:
                        max_rows(X, bX)
                    if there(bY + 1) and n in stack_steps(Y):
                        make_stack(Y, bY + 1, stack_steps(Y).index(n))

            project(SELF, 0, 0)
            project(SELF, 0, 1)
            for g in range(4):
                make_stack(SELF, 0, g)
            slots_of(emit, pe)

        @block.scalar
        def _(act):
            def stack_q(Y, b, g):
                act.wait_ge(tr_mm[Y].sem, tr_mm[Y].count(b, 2 * g + 1))
                if e_mm[Y].due(b - 1, 4 * g + 4):
                    act.wait_ge(e_mm[Y].sem, e_mm[Y].count(b - 1, 4 * g + 4))
                nc.scalar.copy(stack[Y][0:STACK, Q, 4 * g:4 * g + 4, :],
                               ps_t[0:STACK, Q, :, :]).then_inc(tr_evq[Y].sem, 1)

            def split_steps(Y, b, n):
                if n == 0 and tr_mm[Y].due(b - 1):
                    act.wait_ge(tr_mm[Y].sem, tr_mm[Y].count(b - 1))
                for t in range(T2):
                    if n != 1:
                        act.wait_ge(split_p[Y].sem, split_p[Y].count(b, split_p[Y].per - 6 + n + t + 1))
                        slot = n // 2
                        nc.scalar.copy(parts[Y][:, t, :, :, slot * R:(slot + 1) * R],
                                       by_head((qk[Y], rest)[slot], t)).then_inc(split_a[Y].sem, 1)
                    else:
                        put_parts(nc.scalar.copy, Y, t, Q, 0, qk[Y]).then_inc(split_a[Y].sem, 1)

            def exponentials(Y, b, h):
                act.wait_ge(e_mm[Y].sem, e_mm[Y].count(b, h + 1))
                if h >= 4:
                    act.wait_ge(pv_mm[Y].sem, pv_mm[Y].count(b, h - 3))
                elif h == 0:
                    if pv_mm[1 - Y].due(before(Y, b)):
                        act.wait_ge(pv_mm[1 - Y].sem, pv_mm[1 - Y].count(before(Y, b)))
                    if pv_mm[Y].due(b - 1):
                        act.wait_ge(pv_mm[Y].sem, pv_mm[Y].count(b - 1))
                nc.scalar.activation(prob[:, h % 4, :], ps_e[:, h % 2, :, :].rearrange("p t s -> p (t s)"),
                                     ACT.Exp, scale=SCALE).then_inc(e_exp[Y].sem, 1)

            def out_columns(Y, b, g):
                act.wait_ge(pv_mm[Y].sem, pv_mm[Y].count(b, 4 * g + 4))
                if g == 0:
                    if o_mm[Y].due(b - 1):
                        act.wait_ge(o_mm[Y].sem, o_mm[Y].count(b - 1))
                nc.scalar.copy(outT[Y][:, g, :], ps_o[:, 0:S]).then_inc(pv_ev[Y].sem, 1)

            def columns(X, b):
                act.wait_ge(col_mm[X].sem, col_mm[X].count(b))
                if X == SELF:
                    if qk_mm[CROSS].due(b - 1):
                        act.wait_ge(qk_mm[CROSS].sem, qk_mm[CROSS].count(b - 1))
                else:
                    if proj_mm.due(b - 1):
                        act.wait_ge(proj_mm.sem, proj_mm.count(b - 1))
                nc.scalar.copy((x1T if X == SELF else attT)[:, :, :],
                               ps_p[:, :].rearrange("p (k s) -> p k s", k=KD)).then_inc(col_ev[X].sem, 1)

            def x2_columns(b):
                act.wait_ge(x2T_mm.sem, x2T_mm.count(b))
                if r_mm.due(b - 1):
                    act.wait_ge(r_mm.sem, r_mm.count(b - 1))
                nc.scalar.copy(x2T[:, :, :], ps_p[:, :].rearrange("p (k s) -> p k s", k=KD)).then_inc(x2T_ev.sem, 1)

            def emit(i, X, Y, bX, bY):
                for n in range(21):
                    if there(bY) and 4 <= n < H + 4:
                        exponentials(Y, bY, n - 4)
                    if there(bY) and n >= 5 and (n - 5) % 4 == 3:
                        out_columns(Y, bY, (n - 5) // 4)
                    if there(bX - 1) and n == (4 if X == SELF else 5):
                        columns(X, bX - 1)
                    if there(bX - 1) and X == CROSS and n == 10:
                        x2_columns(bX - 1)
                    if there(bY + 1) and n - first_step(Y) in (1, 2, 5):
                        split_steps(Y, bY + 1, (1, 2, 5).index(n - first_step(Y)))
                    if there(bY + 1) and n in stack_steps(Y):
                        stack_q(Y, bY + 1, stack_steps(Y).index(n))

            for n in range(3):
                split_steps(SELF, 0, n)
            for g in range(4):
                stack_q(SELF, 0, g)
            slots_of(emit, act)

        @block.vector
        def _(dve):
            nc.vector.memset(zero[:, :], 0.0).then_inc(zeroed.sem, 1)
            for T in (SELF, CROSS):
                nc.vector.memset(val[T][:, :, :, :], 1.0).then_inc(consts.sem, 1)
                nc.vector.memset(parts[T][:, :, :, :, :], 0.0).then_inc(consts.sem, 1)
                dve.wait_ge(consts.sem, consts.count(0, 3 * T + 2))
                for t in range(T2):
                    nc.vector.memset(parts[T][:, t, Q, :, DATA:MASKED], 1.0)
                    last = nc.vector.memset(parts[T][:, t, K, :, MASKED:STACK], 1.0)
                last.then_inc(consts.sem, 1)
            dve.wait_ge(load_w.sem, load_w.count(0, load_w.per))
            nc.vector.tensor_copy(ident_b[:, :], ident[:, :]).then_inc(consts.sem, 1)
            nc.vector.memset(minus_half[:, :], -0.5).then_inc(consts.sem, 1)
            nc.vector.tensor_copy(mask_f[:, :], mask_i[:, :]).then_inc(masks.sem, 1)
            dve.wait_ge(masks.sem, masks.count(0, 1))
            nc.vector.tensor_scalar(hidden_f[:, :], mask_f[:, :], 0.0, None, ALU.is_equal).then_inc(masks.sem, 1)
            dve.wait_ge(masks.sem, masks.count(0, 2))
            by_tile = hidden_f[:, :].rearrange("p (b t) -> p b t", t=T2)
            nc.vector.tensor_scalar(mask_all[:, :, :, 0], by_tile, -1.0, 1.0, ALU.mult, ALU.add).then_inc(masks.sem, 1)
            for j, part in enumerate(bf16_parts(MASK_VALUE)):
                nc.vector.tensor_scalar(mask_all[:, :, :, 1 + j], by_tile, part, None, ALU.mult).then_inc(masks.sem, 1)

            dve.wait_ge(consts.sem, consts.count(0))

            def maxima(X, b, h):
                dve.wait_ge(s_mm[X].sem, s_mm[X].count(b, h + 1))
                if h == 0:
                    if neg[X].due(b - 1):
                        dve.wait_ge(neg[X].sem, neg[X].count(b - 1))
                    if neg[1 - X].due(before(X, b)):
                        dve.wait_ge(neg[1 - X].sem, neg[1 - X].count(before(X, b)))
                nc.vector.tensor_reduce(smax[:, :, h], ps_s[:, h % 2, :, :], AX.X, ALU.max).then_inc(s_max[X].sem, 1)

            def values(X, b):
                dve.wait_ge(v_mm[X].sem, v_mm[X].count(b))
                if pv_mm[X].due(b - 1):
                    dve.wait_ge(pv_mm[X].sem, pv_mm[X].count(b - 1))
                rows = ps_p[:, :].rearrange("p (t h r) -> p t h r", t=T2, h=H)
                if X == SELF:
                    nc.vector.tensor_copy(val[X][:, :, :, 0:R], rows).then_inc(v_ev[X].sem, 1)
                else:
                    bias = bias_v[:, :].rearrange("p (h r) -> p h r", h=H).unsqueeze(1).to_broadcast([P, T2, H, R])
                    nc.vector.tensor_tensor(val[X][:, :, :, 0:R], rows, bias, ALU.add).then_inc(v_ev[X].sem, 1)

            def queries_keys(Y, b, t):
                dve.wait_ge(qk_mm[Y].sem, qk_mm[Y].count(b, t + 1))
                if split_p[Y].due(b - 1):
                    for split in (split_p, split_a, split_v):
                        dve.wait_ge(split[Y].sem, split[Y].count(b - 1))
                if Y == CROSS:
                    nc.vector.tensor_tensor(qk[Y][:, t, :], ps_p[:, :], bias_qk[:, :], ALU.add)\
                      .then_inc(qk_ev[Y].sem, 1)
                    return
                pairs = ps_p[:, :].rearrange("p (h c r) -> p h c r", c=2, r=R // 2)
                cos = rope_c[:, t, :].unsqueeze(1).to_broadcast([P, 2 * 2 * H, R // 2])
                sin = rope_s[:, t, :].unsqueeze(1).to_broadcast([P, 2 * H, R // 2])
                nc.vector.tensor_tensor(qk[Y][:, t, :].rearrange("p (m r) -> p m r", r=R // 2),
                                        ps_p[:, :].rearrange("p (m r) -> p m r", r=R // 2), cos, ALU.mult)\
                  .then_inc(qk_ev[Y].sem, 1)
                turned = rot[:, t, :].rearrange("p (h c r) -> p h c r", c=2, r=R // 2)
                nc.vector.scalar_tensor_tensor(turned[:, :, 0, :], pairs[:, :, 1, :], -1.0, sin, ALU.mult, ALU.mult)\
                  .then_inc(qk_ev[Y].sem, 1)
                nc.vector.tensor_tensor(turned[:, :, 1, :], pairs[:, :, 0, :], sin, ALU.mult).then_inc(qk_ev[Y].sem, 1)

            def split_steps(Y, b, n):
                if n == 0 and tr_mm[Y].due(b - 1):
                    dve.wait_ge(tr_mm[Y].sem, tr_mm[Y].count(b - 1))
                for t in range(T2):
                    dve.wait_ge(split_p[Y].sem, split_p[Y].count(b, split_p[Y].per - 6 + 2 * n + t + 1))
                    for part in (K,) if n == 0 else (Q, K):
                        put_parts(nc.vector.tensor_copy, Y, t, part, n, (qk[Y], rest, rest2)[n])\
                          .then_inc(split_v[Y].sem, 1)

            def stack_k(Y, b, g):
                dve.wait_ge(tr_mm[Y].sem, tr_mm[Y].count(b, 2 * g + 2))
                if e_mm[Y].due(b - 1, 4 * g + 4):
                    dve.wait_ge(e_mm[Y].sem, e_mm[Y].count(b - 1, 4 * g + 4))
                nc.vector.tensor_copy(stack[Y][0:STACK, K, 4 * g:4 * g + 4, :],
                                      ps_t[0:STACK, K, :, :]).then_inc(tr_evk[Y].sem, 1)

            def max_rows(X, b):
                dve.wait_ge(neg_mm[X].sem, neg_mm[X].count(b))
                if max_in[1 - X].due(before(X, b)):
                    dve.wait_ge(max_in[1 - X].sem, max_in[1 - X].count(before(X, b)))
                if max_in[X].due(b - 1):
                    dve.wait_ge(max_in[X].sem, max_in[X].count(b - 1))
                nc.vector.tensor_copy(nrows[:, :], ps_pb[0:3 * H, 0:S]).then_inc(neg_ev[X].sem, 1)

            def layernorm(X, b, at, rows, st, out):
                s = ln[X]
                dve.wait_ge(s.sem, s.count(b, at))
                for t in range(T2):
                    nc.vector.bn_stats(st[:, t, :], rows[:, t, :]).then_inc(s.sem, 1)
                dve.wait_ge(s.sem, s.count(b, at + 2))
                dve.sem_inc(fences["dve"])
                for t in range(T2):
                    nc.vector.bn_aggr(mv[X][:, t, :], st[:, t, :]).then_inc(s.sem, 1)
                dve.wait_ge(ln_r[X].sem, ln_r[X].count(b))
                for t in range(T2):
                    nc.vector.tensor_scalar(out[:, t, :], rows[:, t, :], mv[X][:, t, 0:1], rstd[X][:, t:t + 1],
                                            ALU.subtract, ALU.mult).then_inc(s.sem, 1)

            def divide(X, b, t):
                s, dst = ln[X], (att, att2)[X]
                dve.wait_ge(o_mm[X].sem, o_mm[X].count(b, t + 1))
                heads = ps_p[:, :].rearrange("p (h r) -> p h r", h=H)
                if t == 0:
                    if col_mm[X].due(b - 1):
                        dve.wait_ge(col_mm[X].sem, col_mm[X].count(b - 1))
                    if s.due(b - 1):
                        dve.wait_ge(s.sem, s.count(b - 1))
                    if ln[1 - X].due(before(X, b)):
                        dve.wait_ge(ln[1 - X].sem, ln[1 - X].count(before(X, b)))
                nc.vector.reciprocal(rden[:, t, :], heads[:, :, R]).then_inc(s.sem, 1)
                dve.wait_ge(s.sem, s.count(b, 2 * t + 1))
                nc.vector.tensor_tensor(dst[:, t, :].rearrange("p (h r) -> p h r", h=H), heads[:, :, 0:R],
                                        rden[:, t, :].unsqueeze(2).to_broadcast([P, H, R]), ALU.mult)\
                  .then_inc(s.sem, 1)

            def first_norm(b):
                dve.wait_ge(res_in.sem, res_in.count(b))
                dve.wait_ge(ln[SELF].sem, ln[SELF].count(b, 4))
                for t in range(T2):
                    nc.vector.tensor_tensor(y[:, t, :], att[:, t, :], x_res[:, t, :], ALU.add).then_inc(ln[SELF].sem, 1)
                if col_mm[SELF].due(b - 1):
                    dve.wait_ge(col_mm[SELF].sem, col_mm[SELF].count(b - 1))
                if x1b_made.due(b - 1):
                    dve.wait_ge(x1b_made.sem, x1b_made.count(b - 1))
                layernorm(SELF, b, 6, y, stats, x1)

            def second_norm(b):
                dve.wait_ge(proj_mm.sem, proj_mm.count(b))
                dve.wait_ge(x1b_made.sem, x1b_made.count(b))
                nc.vector.tensor_tensor(y2[:, :, :].rearrange("p t d -> p (t d)"), ps_p[:, :],
                                        x1b[:, :, :].rearrange("p t d -> p (t d)"), ALU.add).then_inc(ln[CROSS].sem, 1)
                if x2_sent.due(b - 1):
                    dve.wait_ge(x2_sent.sem, x2_sent.count(b - 1))
                if x2T_mm.due(b - 1):
                    dve.wait_ge(x2T_mm.sem, x2T_mm.count(b - 1))
                layernorm(CROSS, b, 5, y2, stats2, x2)

            def routing_logits(b):
                dve.wait_ge(r_mm.sem, r_mm.count(b))
                nc.vector.tensor_tensor(logits[:, bass.ds(b, 1), :, :].rearrange("p b t e -> p (b t) e"),
                                        ps_p[:, 0:T2 * 8].rearrange("p (t e) -> p t e", e=8),
                                        rb[:, :].unsqueeze(1).to_broadcast([P, T2, 8]), ALU.add).then_inc(r_ev.sem, 1)

            def emit(i, X, Y, bX, bY):
                for n in range(21):
                    if there(bX) and n < H:
                        maxima(X, bX, n)
                    if there(bX - 1) and n < 2:
                        divide(X, bX - 1, n)
                    if there(bX) and n == 2:
                        values(X, bX)
                    if there(bX - 1) and X == SELF and n == 2:
                        first_norm(bX - 1)
                    if there(bX - 1) and X == CROSS:
                        if n == 7:
                            second_norm(bX - 1)
                        if n == 12:
                            routing_logits(bX - 1)
                    if there(bY + 1) and n - first_step(Y) in range(T2):
                        queries_keys(Y, bY + 1, n - first_step(Y))
                    if there(bY + 1) and n - first_step(Y) in (3, 6, 8):
                        split_steps(Y, bY + 1, (3, 6, 8).index(n - first_step(Y)))
                    if there(bX) and n == 18:
                        max_rows(X, bX)
                    if there(bY + 1) and n in stack_steps(Y):
                        stack_k(Y, bY + 1, stack_steps(Y).index(n))

            queries_keys(SELF, 0, 0)
            queries_keys(SELF, 0, 1)
            for n in range(3):
                split_steps(SELF, 0, n)
            for g in range(4):
                stack_k(SELF, 0, g)
            slots_of(emit, dve)

        @block.gpsimd
        def _(pool):
            def ready():
                pool.sem_inc(fences["pool"])

            def wholes_and_rests(Y, b):
                tally = Tally()
                if tr_mm[Y].due(b - 1):
                    pool.wait_ge(tr_mm[Y].sem, tr_mm[Y].count(b - 1))
                if Y == CROSS:
                    ready()
                    nc.gpsimd.tensor_copy(mask_now[:, :, :], mask_all[:, bass.ds(b, 1), :, :]
                                          .rearrange("p b t m -> p (b t) m")).then_inc(split_p[Y].sem, 1)
                    pool.wait_ge(split_p[Y].sem, split_p[Y].count(b, tally.one()))
                    ready()
                    for t in range(T2):
                        nc.gpsimd.tensor_copy(parts[Y][:, t, K, :, DATA:MASKED],
                                              mask_now[:, t, 1:4].unsqueeze(1).to_broadcast([P, H, 3]))\
                          .then_inc(split_p[Y].sem, 1)
                        tally.one()
                for t in range(T2):
                    pool.wait_ge(qk_ev[Y].sem, qk_ev[Y].count(b, (t + 1) * qk_ev[Y].per // T2))
                    ready()
                    if Y == SELF:
                        nc.gpsimd.tensor_tensor(qk[Y][:, t, :], qk[Y][:, t, :], rot[:, t, :], ALU.add)\
                          .then_inc(split_p[Y].sem, 1)
                    else:
                        nc.gpsimd.tensor_scalar(qk[Y][:, t, D:2 * D], qk[Y][:, t, D:2 * D], mask_now[:, t, 0:1],
                                                None, ALU.mult).then_inc(split_p[Y].sem, 1)
                    tally.one()
                if split_v[1 - Y].due(before(Y, b)):
                    pool.wait_ge(split_v[1 - Y].sem, split_v[1 - Y].count(before(Y, b)))
                    pool.wait_ge(split_a[1 - Y].sem, split_a[1 - Y].count(before(Y, b)))
                for n, (level, left) in enumerate(((qk[Y], rest), (rest, rest2))):
                    for t in range(T2):
                        pool.wait_ge(split_a[Y].sem, split_a[Y].count(b, 4 * n + t + 1))
                        pool.wait_ge(split_p[Y].sem, split_p[Y].count(b, tally.n - 1))
                        ready()
                        nc.gpsimd.tensor_tensor(by_head(left, t), by_head(level, t),
                                                parts[Y][:, t, :, :, n * R:(n + 1) * R], ALU.subtract)\
                          .then_inc(split_p[Y].sem, 1)
                        tally.one()
                assert tally.n == split_p[Y].per

            def negated_maxima(X, b):
                s = neg[X]
                pool.wait_ge(s_max[X].sem, s_max[X].count(b))
                if neg_mm[X].due(b - 1):
                    pool.wait_ge(neg_mm[X].sem, neg_mm[X].count(b - 1))
                if neg_mm[1 - X].due(before(X, b)):
                    pool.wait_ge(neg_mm[1 - X].sem, neg_mm[1 - X].count(before(X, b)))
                if neg[1 - X].due(before(X, b)):
                    pool.wait_ge(neg[1 - X].sem, neg[1 - X].count(before(X, b)))
                if neg[X].due(b - 1):
                    pool.wait_ge(neg[X].sem, neg[X].count(b - 1))
                ready()
                nc.gpsimd.tensor_scalar(nmax[:, :, :], smax[:, :, :], -1.0, None, ALU.mult).then_inc(s.sem, 1)
                level = nmax
                for j in range(3):
                    pool.wait_ge(s.sem, s.count(b, 1 + 2 * j))
                    ready()
                    nc.gpsimd.tensor_copy(nparts[:, :, j, :], level[:, :, :]).then_inc(s.sem, 1)
                    if j < 2:
                        pool.wait_ge(s.sem, s.count(b, 2 + 2 * j))
                        ready()
                        new = (nrest, nrest2)[j]
                        nc.gpsimd.tensor_tensor(new[:, :, :], level[:, :, :], nparts[:, :, j, :], ALU.subtract)\
                          .then_inc(s.sem, 1)
                        level = new

            def inverse_deviation(X, b):
                pool.wait_ge(ln[X].sem, ln[X].count(b, 10 if X == SELF else 9))
                ready()
                nc.gpsimd.tensor_scalar(veps[X][:, :], mv[X][:, :, 1], EPS, None, ALU.add).then_inc(ln_r[X].sem, 1)
                pool.wait_ge(ln_r[X].sem, ln_r[X].count(b, 1))
                ready()
                nc.gpsimd.tensor_tensor(rstd[X][:, :], veps[X][:, :], minus_half[:, :], ALU.pow).then_inc(ln_r[X].sem, 1)

            def residual_with_bias(b):
                pool.wait_ge(ln[SELF].sem, ln[SELF].count(b))
                if ln[CROSS].due(b - 1, 5):
                    pool.wait_ge(ln[CROSS].sem, ln[CROSS].count(b - 1, 5))
                ready()
                nc.gpsimd.tensor_tensor(x1b[:, :, :], x1[:, :, :], bias_o[:, :].unsqueeze(1).to_broadcast([P, T2, D]),
                                        ALU.add).then_inc(x1b_made.sem, 1)

            def emit(i, X, Y, bX, bY):
                if Y == CROSS:
                    if there(bX - 1):
                        inverse_deviation(X, bX - 1)
                    if there(bY + 1):
                        wholes_and_rests(Y, bY + 1)
                else:
                    if there(bY + 1):
                        wholes_and_rests(Y, bY + 1)
                    if there(bX - 1):
                        inverse_deviation(X, bX - 1)
                    if there(bX):
                        residual_with_bias(bX)
                if there(bX):
                    negated_maxima(X, bX)

            pool.wait_ge(load_w.sem, load_w.count(0, load_w.per))
            pool.wait_ge(consts.sem, consts.count(0))
            pool.wait_ge(masks.sem, masks.count(0))
            ready()
            wholes_and_rests(SELF, 0)
            slots_of(emit, pool)


E = 8
F = 1024
TOP = 2
TILES = 32 * T2
CAP = -(-32 * S * 5 // (E * 4))
ROWS = E * CAP
SKIP = 4 * ROWS
CT = 5
CHUNK = CT * P
CHUNKS = ROWS // CHUNK
HALF = CHUNK // 2
FT = F // P
GT = 4
GROUPS = TILES // GT


CHOSEN = 6 + 5 + 1 + 5 + 4


def routing(nc, logits, tables, slot_s, slot_g, weight):
    ctx = ExitStack()
    with ctx:
        def sb(name, shape, dt=F32):
            return ctx.enter_context(nc.sbuf_tensor(name, shape, dt))

        def sem(name):
            return ctx.enter_context(nc.semaphore(name))

        rank = sb("rank", [P, E])
        first_slot = sb("first_slot", [P, E])
        upto = sb("upto", [P, P], BF16)
        upto_f = sb("upto_f", [P, P])
        ones_b = sb("ones_b", [P, P], BF16)
        ones = sb("ones_t", [P, TILES])
        top = sb("top", [P, TILES])
        gates = sb("gates", [P, TILES, E])
        left = sb("left", [P, TILES, E])
        hit = sb("hit", [P, TILES, E])
        pick = [sb(f"pick{c}", [P, TILES, E]) for c in range(TOP)]
        chosen = sb("chosen", [P, TILES, E], BF16)
        total = sb("total", [P, TILES, E])
        running = sb("running", [P, TILES, E])
        pos = sb("pos", [P, TILES, E])
        valid = sb("valid", [P, TILES, E])
        work = sb("work", [P, TILES, E])
        slot_f = sb("slot_f", [P, TILES])
        valid_f = sb("valid_f", [P, TILES])
        tmp = sb("tmp", [P, TILES])
        ps_within = ctx.enter_context(nc.psum_tensor("ps_within", [P, TILES * E], F32))
        ps_total = ctx.enter_context(nc.psum_tensor("ps_total", [P, TILES * E], F32))
        loaded, step, exp_done, counted = sem("r_loaded"), sem("r_step"), sem("r_exp"), sem("r_counted")
        block = ctx.enter_context(nc.Block())

        @block.sync
        def _(sp):
            sp.dma_start(rank[:, :], tables["rank"].partition_broadcast(P)).then_inc(loaded, 16)
            sp.dma_start(first_slot[:, :], tables["first_slot"].partition_broadcast(P)).then_inc(loaded, 16)
            sp.dma_start(upto_f[:, :], tables["upto"]).then_inc(loaded, 16)

        @block.scalar
        def _(act):
            act.wait_ge(step, 2)
            nc.scalar.activation(gates[:, :, :], left[:, :, :], ACT.Exp).then_inc(exp_done, 1)

        @block.tensor
        def _(pe):
            pe.wait_ge(step, CHOSEN)
            nc.tensor.matmul(ps_within[:, :], upto[:, :], chosen[:, :, :].rearrange("p t e -> p (t e)"),
                             start=True, stop=True)
            nc.tensor.matmul(ps_total[:, :], ones_b[:, :], chosen[:, :, :].rearrange("p t e -> p (t e)"),
                             start=True, stop=True).then_inc(counted, 1)

        @block.vector
        def _(dve):
            tally = Tally()

            def wide(a):
                return a.unsqueeze(2).to_broadcast([P, TILES, E])

            def by_expert(a):
                return a.unsqueeze(1).to_broadcast([P, TILES, E])

            v = nc.vector
            lg = logits[:, :, :, :].rearrange("p b t e -> p (b t) e")
            v.tensor_reduce(top[:, :], lg, AX.X, ALU.max).then_inc(step, 1)
            dve.wait_ge(step, tally.one())
            v.tensor_tensor(left[:, :, :], lg, wide(top[:, :]), ALU.subtract).then_inc(step, 1)
            dve.wait_ge(step, tally.one())
            dve.wait_ge(exp_done, 1)
            v.tensor_reduce(top[:, :], gates[:, :, :], AX.X, ALU.add).then_inc(step, 1)
            dve.wait_ge(step, tally.one())
            v.reciprocal(tmp[:, :], top[:, :]).then_inc(step, 1)
            dve.wait_ge(step, tally.one())
            v.tensor_tensor(gates[:, :, :], gates[:, :, :], wide(tmp[:, :]), ALU.mult).then_inc(step, 1)
            dve.wait_ge(step, tally.one())
            v.tensor_copy(left[:, :, :], gates[:, :, :]).then_inc(step, 1)
            dve.wait_ge(step, tally.one())
            dve.wait_ge(loaded, 48)
            for c in range(TOP):
                v.tensor_reduce(top[:, :], left[:, :, :], AX.X, ALU.max).then_inc(step, 1)
                dve.wait_ge(step, tally.one())
                v.tensor_tensor(hit[:, :, :], left[:, :, :], wide(top[:, :]), ALU.is_equal).then_inc(step, 1)
                dve.wait_ge(step, tally.one())
                v.tensor_tensor(hit[:, :, :], hit[:, :, :], by_expert(rank[:, :]), ALU.mult).then_inc(step, 1)
                dve.wait_ge(step, tally.one())
                v.tensor_reduce(top[:, :], hit[:, :, :], AX.X, ALU.max).then_inc(step, 1)
                dve.wait_ge(step, tally.one())
                v.tensor_tensor(pick[c][:, :, :], hit[:, :, :], wide(top[:, :]), ALU.is_equal).then_inc(step, 1)
                dve.wait_ge(step, tally.one())
                if c == 0:
                    v.scalar_tensor_tensor(left[:, :, :], pick[0][:, :, :], -2.0, left[:, :, :], ALU.mult, ALU.add).then_inc(step, 1)
                    dve.wait_ge(step, tally.one())
            v.memset(ones_b[:, :], 1.0).then_inc(step, 1)
            dve.wait_ge(step, tally.one())
            v.memset(ones[:, :], 1.0).then_inc(step, 1)
            dve.wait_ge(step, tally.one())
            v.tensor_copy(upto[:, :], upto_f[:, :]).then_inc(step, 1)
            dve.wait_ge(step, tally.one())
            v.tensor_tensor(chosen[:, :, :], pick[0][:, :, :], pick[1][:, :, :], ALU.add).then_inc(step, 1)
            dve.wait_ge(step, tally.one())
            assert tally.n == CHOSEN
            dve.wait_ge(counted, 1)
            v.tensor_copy(total[:, :, :].rearrange("p t e -> p (t e)"), ps_total[:, :]).then_inc(step, 1)
            dve.wait_ge(step, tally.one())
            for e in range(E):
                v.tensor_tensor_scan(running[:, :, e], ones[:, :], total[:, :, e], 0.0, ALU.mult, ALU.add).then_inc(step, 1)
                dve.wait_ge(step, tally.one())
            v.tensor_tensor(running[:, :, :], running[:, :, :], total[:, :, :], ALU.subtract).then_inc(step, 1)
            dve.wait_ge(step, tally.one())
            v.scalar_tensor_tensor(pos[:, :, :].rearrange("p t e -> p (t e)"), ps_within[:, :], -1.0,
                                      running[:, :, :].rearrange("p t e -> p (t e)"), ALU.add, ALU.add).then_inc(step, 1)
            dve.wait_ge(step, tally.one())
            v.scalar_tensor_tensor(valid[:, :, :], pos[:, :, :], float(CAP), chosen[:, :, :], ALU.is_lt, ALU.mult).then_inc(step, 1)
            dve.wait_ge(step, tally.one())
            v.tensor_tensor(pos[:, :, :], pos[:, :, :], by_expert(first_slot[:, :]), ALU.add).then_inc(step, 1)
            dve.wait_ge(step, tally.one())
            v.tensor_tensor(gates[:, :, :], gates[:, :, :], valid[:, :, :], ALU.mult).then_inc(step, 1)
            dve.wait_ge(step, tally.one())
            for c in range(TOP):
                for src, dst in ((pos, slot_f[:, :]), (valid, valid_f[:, :]), (gates, weight[:, c, :])):
                    v.tensor_tensor(work[:, :, :], pick[c][:, :, :], src[:, :, :], ALU.mult).then_inc(step, 1)
                    dve.wait_ge(step, tally.one())
                    v.tensor_reduce(dst, work[:, :, :], AX.X, ALU.add).then_inc(step, 1)
                    dve.wait_ge(step, tally.one())
                v.tensor_tensor(slot_f[:, :], slot_f[:, :], valid_f[:, :], ALU.mult).then_inc(step, 1)
                dve.wait_ge(step, tally.one())
                v.tensor_copy(slot_g[:, c, :], slot_f[:, :]).then_inc(step, 1)
                dve.wait_ge(step, tally.one())
                v.tensor_scalar(tmp[:, :], valid_f[:, :], -float(SKIP), float(SKIP), ALU.mult, ALU.add).then_inc(step, 1)
                dve.wait_ge(step, tally.one())
                v.tensor_tensor(slot_f[:, :], slot_f[:, :], tmp[:, :], ALU.add).then_inc(step, 1)
                dve.wait_ge(step, tally.one())
                v.tensor_copy(slot_s[:, c, :], slot_f[:, :]).then_inc(step, 1)
                dve.wait_ge(step, tally.one())


def in_pairs(eng, n, emit):
    emit(0, 0)
    emit(1, 1)
    with eng.Fori(1, n // 2 - 1) as i:
        emit(i * 2, 0)
        emit(i * 2 + 1, 1)
    emit(n - 2, 0)
    emit(n - 1, 1)


class Turns:

    def __init__(self, sems, per):
        self.sems, self.per = sems, per

    def count(self, q, parity):
        return q * (self.per // 2) + (self.per - parity * (self.per // 2))

    def due(self, q):
        return not isinstance(q, int) or q >= 0


def dispatch(nc, x2_dram, slots, slot_s):
    with ExitStack() as ctx:
        rows = ctx.enter_context(nc.sbuf_tensor("d_rows", [P, 2, GT, D], F32))
        index = ctx.enter_context(nc.sbuf_tensor("d_index", [P, 2, TOP, GT], U32))

        def sem(name):
            return ctx.enter_context(nc.semaphore(name))

        come = Turns([sem("d_come0"), sem("d_come1")], 16)
        gone = Turns([sem("d_gone0"), sem("d_gone1")], 16 * TOP * GT)
        staged = Steps(sem("d_staged"), 1)
        fence = sem("d_fence")
        block = ctx.enter_context(nc.Block())

        @block.sync
        def _(sp):
            def load(q, u):
                if gone.due(q - 2):
                    sp.wait_ge(gone.sems[u], gone.count(q - 2, u))
                sp.dma_start(rows[:, u, :, :], x2_dram[bass.ds(q * (GT * P), GT * P), :]
                             .rearrange("(g p) d -> p g d", p=P)).then_inc(come.sems[u], 16)
            in_pairs(sp, GROUPS, load)

        @block.vector
        def _(dve):
            def stage(q, u):
                if gone.due(q - 2):
                    dve.wait_ge(gone.sems[u], gone.count(q - 2, u))
                nc.vector.tensor_copy(index[:, u, :, :], slot_s[:, :, bass.ds(q * GT, GT)]).then_inc(staged.sem, 1)
            in_pairs(dve, GROUPS, stage)

        @block.gpsimd
        def _(pool):
            def scatter(q, u):
                pool.wait_ge(staged.sem, staged.count(q))
                pool.wait_ge(come.sems[u], come.count(q, u))
                pool.sem_inc(fence)
                for g in range(GT):
                    for c in range(TOP):
                        nc.gpsimd.indirect_dma_start(
                            out=slots[:, :], out_offset=bass.IndirectOffsetOnAxis(ap=index[:, u, c, g:g + 1], axis=0),
                            in_=rows[:, u, g, :], in_offset=None, bounds_check=ROWS - 1, oob_is_err=False,
                        ).then_inc(gone.sems[u], 16)
            in_pairs(pool, GROUPS, scatter)
            for u in range(2):
                pool.wait_ge(gone.sems[u], gone.count(GROUPS - 2 + u, u))


def experts(nc, slots, results, ident_dram, w1, b1, w2, b2):
    per_expert = CAP // CHUNK
    with ExitStack() as ctx:
        def sb(name, shape, dt=F32):
            return ctx.enter_context(nc.sbuf_tensor(name, shape, dt))

        def sem(name):
            return ctx.enter_context(nc.semaphore(name))

        ident = sb("m_ident", [P, P])
        w1_sb = sb("w1_sb", [P, 2, KD, F])
        w2_sb = sb("w2_sb", [P, 2, FT, D])
        b1_sb = sb("b1_sb", [P, 2, FT])
        b2_sb = sb("b2_sb", [P, 2, D])
        rows = sb("m_rows", [P, 2, CT, D])
        cols = sb("m_cols", [P, 2, KD, CHUNK])
        hid = sb("hid", [P, FT, CHUNK])
        res = sb("m_res", [P, 2, CT, D])
        ps_t = ctx.enter_context(nc.psum_tensor("m_ps_t", [P, 2, 512], F32))
        ps_h = ctx.enter_context(nc.psum_tensor("m_ps_h", [P, 4, 512], F32))
        ps_o = ctx.enter_context(nc.psum_tensor("m_ps_o", [P, 2, 512], F32))

        id_in = sem("m_id")
        w_in = Turns([sem("w_in0"), sem("w_in1")], 64)
        rows_in = Turns([sem("m_rows_in0"), sem("m_rows_in1")], 16)
        sent = Turns([sem("m_sent0"), sem("m_sent1")], 16)
        t_mm = Steps(sem("m_t_mm"), CT)
        t_ev = Steps(sem("m_t_ev"), CT)
        h_mm = Steps(sem("m_h_mm"), 2 * FT)
        h_ev = Steps(sem("m_h_ev"), 2 * FT)
        o_mm = Steps(sem("m_o_mm"), CT)
        o_ev = Steps(sem("m_o_ev"), CT)
        fence = sem("m_fence")
        block = ctx.enter_context(nc.Block())

        def turns(eng, emit):
            def four(i):
                for u in range(4):
                    emit(i * 4 + u, i * 2 + u // per_expert, u % 2, u // per_expert)
            four(0)
            with eng.Fori(1, CHUNKS // 4 - 1) as i:
                four(i)
            four(CHUNKS // 4 - 1)

        @block.sync
        def _(sp):
            sp.dma_start(ident[:, :], ident_dram).then_inc(id_in, 16)

            def load(q, e, u, pe_):
                if u == 0:
                    if o_ev.due(q - 3):
                        sp.wait_ge(o_ev.sem, o_ev.count(q - 3))
                    for dst, a in ((w1_sb[:, pe_, :, :], w1[bass.ds(e, 1), :, :].rearrange("e (k p) f -> p (e k) f", p=P)),
                                   (w2_sb[:, pe_, :, :], w2[bass.ds(e, 1), :, :].rearrange("e (k p) d -> p (e k) d", p=P)),
                                   (b1_sb[:, pe_, :], b1[bass.ds(e, 1), :, :].rearrange("e p k -> p (e k)")),
                                   (b2_sb[:, pe_, :], b2[bass.ds(e, 1), :].to_broadcast([P, D]))):
                        sp.dma_start(dst, a).then_inc(w_in.sems[pe_], 16)
                if t_mm.due(q - 2):
                    sp.wait_ge(t_mm.sem, t_mm.count(q - 2))
                sp.dma_start(rows[:, u, :, :], slots[bass.ds(q * CHUNK, CHUNK), :].rearrange("(c p) d -> p c d", p=P))\
                  .then_inc(rows_in.sems[u], 16)
            turns(sp, load)

        @block.gpsimd
        def _(pool):
            def store(q, e, u, pe_):
                pool.wait_ge(o_ev.sem, o_ev.count(q))
                if sent.due(q - 2):
                    pool.wait_ge(sent.sems[u], sent.count(q - 2, u))
                pool.sem_inc(fence)
                pool.dma_start(results[bass.ds(q * CHUNK, CHUNK), :].rearrange("(c p) d -> p c d", p=P),
                               res[:, u, :, :]).then_inc(sent.sems[u], 16)
            turns(pool, store)
            for u in range(2):
                pool.wait_ge(sent.sems[u], sent.count(CHUNKS - 2 + u, u))
        @block.tensor
        def _(pe):
            pe.wait_ge(id_in, 16)

            def to_columns(q, u):
                pe.wait_ge(rows_in.sems[u], rows_in.count(q, u))
                for c in range(CT):
                    if c >= 2:
                        pe.wait_ge(t_ev.sem, t_ev.count(q, c - 1))
                    elif c == 0:
                        if t_ev.due(q - 1):
                            pe.wait_ge(t_ev.sem, t_ev.count(q - 1))
                    for k in range(KD):
                        mm = nc.tensor.transpose(ps_t[:, c % 2, k * P:(k + 1) * P], rows[:, u, c, k * P:(k + 1) * P],
                                                 ident[:, :])
                    mm.then_inc(t_mm.sem, 1)

            def hidden(q, u, pe_, e):
                if u == 0:
                    pe.wait_ge(w_in.sems[pe_], w_in.count(e, pe_))
                pe.wait_ge(t_ev.sem, t_ev.count(q))
                for m in range(FT):
                    for half in range(2):
                        n = 2 * m + half
                        if n >= 4:
                            pe.wait_ge(h_ev.sem, h_ev.count(q, n - 3))
                        elif n == 0:
                            if h_ev.due(q - 1):
                                pe.wait_ge(h_ev.sem, h_ev.count(q - 1))
                        for k in range(KD):
                            mm = nc.tensor.matmul(ps_h[:, n % 4, 0:HALF], w1_sb[:, pe_, k, m * P:(m + 1) * P],
                                                  cols[:, u, k, half * HALF:(half + 1) * HALF],
                                                  start=(k == 0), stop=(k == KD - 1))
                        mm.then_inc(h_mm.sem, 1)

            def output(q, pe_):
                pe.wait_ge(h_ev.sem, h_ev.count(q))
                for c in range(CT):
                    if c >= 2:
                        pe.wait_ge(o_ev.sem, o_ev.count(q, c - 1))
                    elif c == 0:
                        if o_ev.due(q - 1):
                            pe.wait_ge(o_ev.sem, o_ev.count(q - 1))
                    for k in range(FT):
                        mm = nc.tensor.matmul(ps_o[:, c % 2, 0:D], hid[:, k, c * P:(c + 1) * P], w2_sb[:, pe_, k, :],
                                              start=(k == 0), stop=(k == FT - 1))
                    mm.then_inc(o_mm.sem, 1)

            def emit(q, e, u, pe_):
                hidden(q, u, pe_, e)
                if not isinstance(q, int) or q + 1 < CHUNKS:
                    to_columns(q + 1, 1 - u)
                output(q, pe_)
            to_columns(0, 0)
            turns(pe, emit)

        @block.scalar
        def _(act):
            def emit(q, e, u, pe_):
                if u == 0:
                    act.wait_ge(w_in.sems[pe_], w_in.count(e, pe_))
                for m in range(FT):
                    for half in range(2):
                        act.wait_ge(h_mm.sem, h_mm.count(q, 2 * m + half + 1))
                        if m == half == 0:
                            if o_mm.due(q - 1):
                                act.wait_ge(o_mm.sem, o_mm.count(q - 1))
                        nc.scalar.activation(hid[:, m, half * HALF:(half + 1) * HALF], ps_h[:, (2 * m + half) % 4, 0:HALF],
                                             ACT.Gelu, bias=b1_sb[:, pe_, m:m + 1]).then_inc(h_ev.sem, 1)
            turns(act, emit)

        @block.vector
        def _(dve):
            def columns(q, u):
                for c in range(CT):
                    dve.wait_ge(t_mm.sem, t_mm.count(q, c + 1))
                    if c == 0:
                        if h_mm.due(q - 2):
                            dve.wait_ge(h_mm.sem, h_mm.count(q - 2))
                    nc.vector.tensor_copy(cols[:, u, :, c * P:(c + 1) * P],
                                          ps_t[:, c % 2, 0:D].rearrange("p (k s) -> p k s", k=KD)).then_inc(t_ev.sem, 1)

            def emit(q, e, u, pe_):
                if not isinstance(q, int) or q + 1 < CHUNKS:
                    columns(q + 1, 1 - u)
                if u == 0:
                    dve.wait_ge(w_in.sems[pe_], w_in.count(e, pe_))
                if sent.due(q - 2):
                    dve.wait_ge(sent.sems[u], sent.count(q - 2, u))
                for c in range(CT):
                    dve.wait_ge(o_mm.sem, o_mm.count(q, c + 1))
                    nc.vector.tensor_tensor(res[:, u, c, :], ps_o[:, c % 2, 0:D], b2_sb[:, pe_, :], ALU.add)\
                      .then_inc(o_ev.sem, 1)
            columns(0, 0)
            turns(dve, emit)


def combine(nc, x2_dram, results, slot_g, weight, out):
    with ExitStack() as ctx:
        def sb(name, shape, dt=F32):
            return ctx.enter_context(nc.sbuf_tensor(name, shape, dt))

        def sem(name):
            return ctx.enter_context(nc.semaphore(name))

        index = sb("c_index", [P, 2, TOP, GT], U32)
        w_now = sb("c_weight", [P, 2, TOP, GT])
        rows = sb("c_rows", [P, 2, GT, D])
        got = [sb(f"c_got{c}", [P, 2, GT, D]) for c in range(TOP)]
        stats = sb("c_stats", [P, 2, GT, 6])
        mv = sb("c_mv", [P, 2, GT, 2])
        veps = sb("c_veps", [P, 2, GT])
        rstd = sb("c_rstd", [P, 2, GT])
        minus_half = sb("c_minus_half", [P, GT])
        done = sb("c_done", [P, 2, GT, D])
        come = Turns([sem("c_come0"), sem("c_come1")], 16)
        fetched = Turns([sem("c_got0s"), sem("c_got1s")], 16 * TOP * GT)
        sent = Turns([sem("c_sent0"), sem("c_sent1")], 16)
        staged = Steps(sem("c_staged"), 2)
        summed = Steps(sem("c_summed"), 5 * GT)
        inv = Steps(sem("c_inv"), 2)
        const = sem("c_const")
        fences = [sem("c_fence_pool"), sem("c_fence_dve")]
        block = ctx.enter_context(nc.Block())
        out_rows = out.rearrange("b s d -> (b s) d")

        @block.sync
        def _(sp):
            def load(q, u):
                if summed.due(q - 2, TOP * GT):
                    sp.wait_ge(summed.sem, summed.count(q - 2, TOP * GT))
                sp.dma_start(rows[:, u, :, :], x2_dram[bass.ds(q * (GT * P), GT * P), :]
                             .rearrange("(g p) d -> p g d", p=P)).then_inc(come.sems[u], 16)
            in_pairs(sp, GROUPS, load)

        @block.scalar
        def _(act):
            def store(q, u):
                act.wait_ge(summed.sem, summed.count(q))
                if sent.due(q - 2):
                    act.wait_ge(sent.sems[u], sent.count(q - 2, u))
                act.dma_start(out_rows[bass.ds(q * (GT * P), GT * P), :].rearrange("(g p) d -> p g d", p=P),
                              done[:, u, :, :]).then_inc(sent.sems[u], 16)
            in_pairs(act, GROUPS, store)
            for u in range(2):
                act.wait_ge(sent.sems[u], sent.count(GROUPS - 2 + u, u))

        @block.gpsimd
        def _(pool):
            pool.memset(minus_half[:, :], -0.5).then_inc(const, 1)

            def gather(q, u):
                pool.wait_ge(staged.sem, staged.count(q))
                if summed.due(q - 2, TOP * GT):
                    pool.wait_ge(summed.sem, summed.count(q - 2, TOP * GT))
                pool.sem_inc(fences[0])
                for g in range(GT):
                    for c in range(TOP):
                        nc.gpsimd.indirect_dma_start(
                            out=got[c][:, u, g, :], out_offset=None, in_=results[:, :],
                            in_offset=bass.IndirectOffsetOnAxis(ap=index[:, u, c, g:g + 1], axis=0),
                            bounds_check=ROWS - 1, oob_is_err=False,
                        ).then_inc(fetched.sems[u], 16)

            def inverse_deviation(q, u):
                pool.wait_ge(summed.sem, summed.count(q, 4 * GT))
                pool.wait_ge(const, 1)
                pool.sem_inc(fences[0])
                nc.gpsimd.tensor_scalar(veps[:, u, :], mv[:, u, :, 1], EPS, None, ALU.add).then_inc(inv.sem, 1)
                pool.wait_ge(inv.sem, inv.count(q, 1))
                pool.sem_inc(fences[0])
                nc.gpsimd.tensor_tensor(rstd[:, u, :], veps[:, u, :], minus_half[:, :], ALU.pow).then_inc(inv.sem, 1)

            def emit(q, u):
                if not isinstance(q, int) or q + 1 < GROUPS:
                    gather(q + 1, 1 - u)
                inverse_deviation(q, u)
            gather(0, 0)
            in_pairs(pool, GROUPS, emit)

        @block.vector
        def _(dve):
            def stage(q, u):
                if fetched.due(q - 2):
                    dve.wait_ge(fetched.sems[u], fetched.count(q - 2, u))
                if summed.due(q - 2):
                    dve.wait_ge(summed.sem, summed.count(q - 2))
                nc.vector.tensor_copy(index[:, u, :, :], slot_g[:, :, bass.ds(q * GT, GT)]).then_inc(staged.sem, 1)
                nc.vector.tensor_copy(w_now[:, u, :, :], weight[:, :, bass.ds(q * GT, GT)]).then_inc(staged.sem, 1)

            def emit(q, u):
                if not isinstance(q, int) or q + 1 < GROUPS:
                    stage(q + 1, 1 - u)
                dve.wait_ge(come.sems[u], come.count(q, u))
                dve.wait_ge(fetched.sems[u], fetched.count(q, u))
                dve.wait_ge(staged.sem, staged.count(q))
                for c in range(TOP):
                    if c:
                        dve.wait_ge(summed.sem, summed.count(q, c * GT))
                    for g in range(GT):
                        nc.vector.scalar_tensor_tensor(got[c][:, u, g, :], got[c][:, u, g, :], w_now[:, u, c, g:g + 1],
                                                       (rows if c == 0 else got[0])[:, u, g, :], ALU.mult, ALU.add)\
                          .then_inc(summed.sem, 1)
                dve.wait_ge(summed.sem, summed.count(q, TOP * GT))
                for g in range(GT):
                    nc.vector.bn_stats(stats[:, u, g, :], got[1][:, u, g, :]).then_inc(summed.sem, 1)
                dve.wait_ge(summed.sem, summed.count(q, 3 * GT))
                dve.sem_inc(fences[1])
                for g in range(GT):
                    nc.vector.bn_aggr(mv[:, u, g, :], stats[:, u, g, :]).then_inc(summed.sem, 1)
                dve.wait_ge(inv.sem, inv.count(q))
                if sent.due(q - 2):
                    dve.wait_ge(sent.sems[u], sent.count(q - 2, u))
                for g in range(GT):
                    nc.vector.tensor_scalar(done[:, u, g, :], got[1][:, u, g, :], mv[:, u, g, 0:1], rstd[:, u, g:g + 1],
                                            ALU.subtract, ALU.mult).then_inc(summed.sem, 1)
            stage(0, 0)
            in_pairs(dve, GROUPS, emit)


def rope_tables():
    inverse = (1.0 / 10000.0 ** (np.arange(0, R, 2, dtype=np.float32) / np.float32(R))).astype(np.float32)
    angle = np.outer(np.arange(S, dtype=np.float32), inverse).astype(np.float32)
    return np.cos(angle), np.sin(angle)


def program(nc, a, out):
    NB = 32
    x2_dram = nc.dram_tensor("x2_dram", (NB, S, D), F32).ap()
    slots = nc.dram_tensor("slots_dram", (ROWS, D), F32).ap()
    results = nc.dram_tensor("results_dram", (ROWS, D), F32).ap()
    x2_rows = x2_dram.rearrange("b s d -> (b s) d")
    with ExitStack() as ctx:
        slot_s = ctx.enter_context(nc.sbuf_tensor("slot_s", [P, TOP, TILES], U32))
        slot_g = ctx.enter_context(nc.sbuf_tensor("slot_g", [P, TOP, TILES], U32))
        weight = ctx.enter_context(nc.sbuf_tensor("weight", [P, TOP, TILES], F32))
        logits = ctx.enter_context(nc.sbuf_tensor("logits", [P, NB, T2, E], F32))
        attention(nc, a["x"], a["xT"], a["ctxT"], a["mask"], {"qk": a["s_qk"], "v": a["s_v"]},
                  {"q": a["c_q"], "k": a["c_k"], "v": a["c_v"], "o": a["c_o"]},
                  {"q": a["b_q"], "k": a["b_k"], "v": a["b_v"], "o": a["b_o"]},
                  {"cos": a["cos"], "sin": a["sin"], "ident": a["ident"]},
                  {"w": a["r_w"], "b": a["r_b"]}, x2_dram, slots, logits, NB)
        routing(nc, logits, a, slot_s, slot_g, weight)
        dispatch(nc, x2_rows, slots, slot_s)
        experts(nc, slots, results, a["ident"], a["w1"], a["b1"], a["w2"], a["b2"])
        combine(nc, x2_rows, results, slot_g, weight, out)


def kernel(**inputs):
    from concourse import bacc
    from concourse.bass_utils import run_bass_kernel_spmd

    def array(name):
        return np.asarray(inputs[name])

    def halves(w):
        return w.reshape(H, R // 2, 2, D).transpose(0, 2, 1, 3).reshape(D, D)

    cos, sin = rope_tables()
    arrays = {
        "x": array("x"),
        "xT": array("x").transpose(0, 2, 1),
        "ctxT": array("ctx_1024").transpose(0, 2, 1),
        "mask": array("mask_Bx1x1xS2_ik0").reshape(32, T2, P).transpose(2, 0, 1).reshape(P, 32 * T2),
        "s_qk": np.concatenate([halves(array("L0_attn_wq")), halves(array("L0_attn_wk"))], 0).T,
        "s_v": array("L0_attn_wv").T,
        "c_q": array("L0_xattn_Wq").T,
        "c_k": array("L0_xattn_Wk").T,
        "c_v": array("L0_xattn_Wv").T,
        "c_o": array("L0_xattn_Wo").T,
        "b_q": array("L0_xattn_bq"),
        "b_k": array("L0_xattn_bk"),
        "b_v": array("L0_xattn_bv"),
        "b_o": array("L0_xattn_bo"),
        "r_w": array("L0_ffn_router_w"),
        "r_b": array("L0_ffn_router_b"),
        "w1": array("L0_ffn_w1"),
        "b1": array("L0_ffn_b1").reshape(E, FT, P).transpose(0, 2, 1),
        "w2": array("L0_ffn_w2"),
        "b2": array("L0_ffn_b2"),
        "cos": cos,
        "sin": sin,
        "ident": np.eye(P, dtype=np.float32),
        "upto": np.triu(np.ones((P, P), np.float32)),
        "rank": np.arange(E, 0, -1).astype(np.float32),
        "first_slot": (np.arange(E) * CAP).astype(np.float32),
    }
    nc = bacc.Bacc("TRN2", target_bir_lowering=False, num_devices=1)
    a, given = {}, {}
    for name, value in arrays.items():
        value = np.ascontiguousarray(value)
        given[f"in_{name}"] = value
        a[name] = nc.dram_tensor(f"in_{name}", value.shape, mybir.dt.from_np(value.dtype), kind="ExternalInput").ap()
    out = nc.dram_tensor("out_0", (32, S, D), F32, kind="ExternalOutput").ap()
    program(nc, a, out)
    result = run_bass_kernel_spmd(nc, [given], core_ids=[0])
    return result.results[0]["out_0"]
```

```python
from contextlib import ExitStack

import numpy as np

import concourse.bass as bass
from concourse import mybir

F32 = mybir.dt.float32
BF16 = mybir.dt.bfloat16
U32 = mybir.dt.uint32
I32 = mybir.dt.int32
ALU = mybir.AluOpType
ACT = mybir.ActivationFunctionType
AX = mybir.AxisListType

P = 128
D = 256
H = 16
R = D // H
S = 256
T2 = S // P
KD = D // P
SLOTS = 6
DATA = SLOTS * R
MASKED = DATA + 3
STACK = MASKED + 3
SCALE = 1.0 / 4.0
MASK_VALUE = -1.0e9 / SCALE
EPS = 1e-5
SELF, CROSS = 0, 1
Q, K = 0, 1
PART_SLOTS = {Q: [(0, 2, 4), (1, 3), (5,)], K: [(0, 3, 5), (1, 2), (4,)]}


def bf16_parts(value):
    parts, rest = [], np.float32(value)
    for _ in range(3):
        part = (np.float32(rest).reshape(1).view(np.uint32) & np.uint32(0xFFFF0000)).view(np.float32)[0]
        parts.append(float(part))
        rest = np.float32(rest - part)
    assert rest == 0
    return parts


class Steps:

    def __init__(self, sem, per):
        self.sem, self.per = sem, per

    def count(self, b, k=None):
        return b * self.per + (self.per if k is None else k)

    def due(self, b, k=None):
        value = self.count(b, k)
        return not isinstance(value, int) or value > 0


class Tally:

    def __init__(self):
        self.n = 0

    def one(self):
        self.n += 1
        return self.n


def attention(nc, x_rows, x_cols, ctx_cols, mask_cols, w_self, w_cross, biases, tables, router, x2_out,
              slots, logits, NB):
    ctx = ExitStack()
    with ctx:
        def sb(name, shape, dt=F32):
            return ctx.enter_context(nc.sbuf_tensor(name, shape, dt))

        def steps(name, per):
            return Steps(ctx.enter_context(nc.semaphore(name)), per)

        def both(name, per_self, per_cross=None):
            return [steps(name + "_self", per_self), steps(name + "_cross", per_cross or per_self)]

        wqk = [sb(f"wqk{t}", [P, KD, 2 * D]) for t in (SELF, CROSS)]
        wv = [sb(f"wv{t}", [P, KD, D]) for t in (SELF, CROSS)]
        wo = sb("wo", [P, KD, D])
        rw = sb("rw", [P, KD, 8])
        rb = sb("rb", [P, 8])
        bias_qk = sb("bias_qk", [P, 2 * D])
        bias_v = sb("bias_v", [P, D])
        bias_o = sb("bias_o", [P, D])
        rope_c = sb("rope_c", [P, T2, R // 2])
        rope_s = sb("rope_s", [P, T2, R // 2])
        ident = sb("ident", [P, P])
        ident_b = sb("ident_b", [P, P], BF16)
        mask_i = sb("mask_i", [P, 32 * T2], I32)
        mask_f = sb("mask_f", [P, 32 * T2])
        hidden_f = sb("hidden_f", [P, 32 * T2])
        mask_all = sb("mask_all", [P, 32, T2, 4])
        mask_now = sb("mask_now", [P, T2, 4])
        src = [sb("xT", [P, KD, S]), sb("ctxT", [P, KD, S])]
        x_res = sb("x_res", [P, T2, D])
        qk = [sb(f"qk{t}", [P, T2, 2 * D]) for t in (SELF, CROSS)]
        rot = sb("rot", [P, T2, 2 * D])
        rest = sb("rest", [P, T2, 2 * D])
        rest2 = sb("rest2", [P, T2, 2 * D])
        parts = [sb(f"parts{t}", [P, T2, 2, H, STACK], BF16) for t in (SELF, CROSS)]
        stack = [sb(f"stack{t}", [P, 2, H, S], BF16) for t in (SELF, CROSS)]
        val = [sb(f"val{t}", [P, T2, H, 32]) for t in (SELF, CROSS)]
        smax = sb("smax", [P, T2, H])
        nmax = sb("nmax", [P, T2, H])
        nrest = sb("nrest", [P, T2, H])
        nrest2 = sb("nrest2", [P, T2, H])
        nparts = sb("nparts", [P, T2, 3, H], BF16)
        nrows = sb("nrows", [3 * H, S], BF16)
        prob = sb("prob", [P, 4, 2 * S])
        outT = [sb(f"outT{t}", [P, 4, S]) for t in (SELF, CROSS)]
        rden = sb("rden", [P, T2, H])
        att = sb("att", [P, T2, D])
        y = sb("y", [P, T2, D])
        stats = sb("stats", [P, T2, 6])
        mv = [sb(f"mv{t}", [P, T2, 2]) for t in (SELF, CROSS)]
        rstd = [sb(f"rstd{t}", [P, T2]) for t in (SELF, CROSS)]
        veps = [sb(f"veps{t}", [P, T2]) for t in (SELF, CROSS)]
        minus_half = sb("minus_half", [P, T2])
        x1 = sb("x1", [P, T2, D])
        x1b = sb("x1b", [P, T2, D])
        x1T = sb("x1T", [P, KD, S])
        att2 = sb("att2", [P, T2, D])
        attT = sb("attT", [P, KD, S])
        y2 = sb("y2", [P, T2, D])
        stats2 = sb("stats2", [P, T2, 6])
        x2 = sb("x2", [P, T2, D])
        x2T = sb("x2T", [P, KD, S])
        zero = sb("zero", [P, 8 * D])
        ps_s = ctx.enter_context(nc.psum_tensor("ps_s", [P, 2, T2, S], F32))
        ps_e = ctx.enter_context(nc.psum_tensor("ps_e", [P, 2, T2, S], F32))
        ps_o = ctx.enter_context(nc.psum_tensor("ps_o", [P, 512], F32))
        ps_w = ctx.enter_context(nc.psum_tensor("ps_w", [P, 3, 512], F32))
        ps_wb = ps_w[:, :, :].bitcast(BF16)

        load_w = steps("load_w", 16 * 16)
        src_in = both("src_in", 16)
        res_in = steps("res_in", 16)
        max_in = both("max_in", 48)
        x2_sent = steps("x2_sent", 16)
        consts = steps("consts", 8)
        masks = steps("masks", 6)
        zeroed = steps("zeroed", 1)
        slots_zero = ctx.enter_context(nc.semaphore("slots_zero"))
        v_mm = both("v_mm", 1)
        v_ev = both("v_ev", 1)
        qk_mm = both("qk_mm", 2)
        qk_ev = both("qk_ev", 6, 2)
        split_p = both("split_p", 6, 9)
        split_a = both("split_a", 6)
        split_v = both("split_v", 10)
        tr_mm = both("tr_mm", 8)
        tr_evq = both("tr_evq", 4)
        tr_evk = both("tr_evk", 4)
        s_mm = both("s_mm", 16)
        s_max = both("s_max", 16)
        neg = both("neg", 6)
        neg_mm = both("neg_mm", 1)
        neg_ev = both("neg_ev", 1)
        e_mm = both("e_mm", 16)
        e_exp = both("e_exp", 16)
        pv_mm = both("pv_mm", 16)
        pv_ev = both("pv_ev", 4)
        o_mm = both("o_mm", 2)
        ln = both("ln", 12, 11)
        ln_r = both("ln_r", 2)
        col_mm = both("col_mm", 1)
        col_ev = both("col_ev", 1)
        proj_mm = steps("proj_mm", 1)
        x1b_made = steps("x1b_made", 1)
        x2T_mm = steps("x2T_mm", 1)
        x2T_ev = steps("x2T_ev", 1)
        r_mm = steps("r_mm", 1)
        r_ev = steps("r_ev", 1)
        fences = {e: ctx.enter_context(nc.semaphore("fence_" + e)) for e in ("pool", "pe", "dve")}

        def slots_of(emit, eng, loop_first=3):
            def step(i):
                emit(i, SELF, CROSS, i, i - 2)
                emit(i, CROSS, SELF, i - 1, i)
            last_full = NB - 2
            first = min(loop_first, NB + 2)
            for i in range(first):
                step(i)
            if first <= last_full:
                with eng.Fori(first, last_full + 1) as i:
                    step(i)
                first = last_full + 1
            for i in range(first, NB + 2):
                step(i)

        def there(b):
            return not isinstance(b, int) or 0 <= b < NB

        def before(T, b):
            other = b - 2 if T == SELF else b + 1
            return min(other, NB - 1) if isinstance(other, int) else other

        def by_head(a, t):
            return a[:, t, :].rearrange("p (c h r) -> p c h r", c=2, h=H)

        def put_parts(copy, Y, t, part, n, level):
            more = [x for x in PART_SLOTS[part][n] if n == 2 or x != n]
            slots = parts[Y][:, t, part, :, 0:DATA].rearrange("p h (s r) -> p h s r", r=R)
            return copy(slots[:, :, more[0]:more[-1] + 1:2, :], by_head(level, t)[:, part]
                        .unsqueeze(2).to_broadcast([P, H, len(more), R]))

        at = [dict(out_rows=(1, 2), values=(11, 12), norm=3, normed=5, columns=6, max_rows=18),
              dict(out_rows=(2, 3), values=(0, 1), columns=5, project_out=(8, 10), norm=10, normed=12, x2_columns=14,
                   route=16, max_rows=18)]
        for_y = [dict(project=(3, 4, 6, 7), split_a=(6, 9, 10, 11, 12), split_v=(6, 9, 10, 11, 12, 13),
                      stack=(15, 16, 18, 19)),
                 dict(project=(5, 6, 7, 8), split_a=(9, 10, 11, 12, 13), split_v=(10, 11, 13, 14, 15, 16),
                      stack=(17, 18, 19, 20))]

        uses = []
        for X, Y in ((SELF, CROSS), (CROSS, SELF)):
            first_use = len(uses)
            for n in range(21):
                for name in ("out_rows", "values", "columns", "project_out", "x2_columns", "route"):
                    where = at[X].get(name, ())
                    if name == "out_rows" and n in where:
                        uses.append((name, X, where.index(n)))
                    elif n == where or name in ("values", "project_out") and where and n == where[0]:
                        uses.append((name, X, 0))
                if n in for_y[Y]["project"][::2]:
                    uses.append(("project", Y, for_y[Y]["project"].index(n) // 2))
                if n == at[X]["max_rows"]:
                    uses.append(("max_rows", X, 0))
                if n in for_y[Y]["stack"]:
                    g = for_y[Y]["stack"].index(n)
                    uses += [("stack_q", Y, g), ("stack_k", Y, g)]

        def bank(name, T, k=0):
            return uses.index((name, T, k)) % 3

        def work(name, T, k=0):
            return ps_w[:, bank(name, T, k), :]

        def work_b(name, T, k=0):
            return ps_wb[:, bank(name, T, k), :]

        def reader(name, T, b, k=0):
            return {
                "out_rows": (ln[T], b, 2 + 2 * k), "values": (v_ev[T], b, 1), "columns": (col_ev[T], b, 1),
                "project_out": (ln[CROSS], b, 5), "x2_columns": (x2T_ev, b, 1), "route": (r_ev, b, 1),
                "project": (qk_ev[T], b, (k + 1) * qk_ev[T].per // T2), "max_rows": (neg_ev[T], b, 1),
                "stack_q": (tr_evq[T], b, k + 1), "stack_k": (tr_evk[T], b, k + 1),
            }[name]

        def readers_after(i):
            found = {}
            for name, T, k in uses[first_use:]:
                b = i + 1 if T == SELF else i - 1 if name in ("values", "max_rows") else i - 2
                found[bank(name, T, k)] = reader(name, T, b, k)
            return found

        block = ctx.enter_context(nc.Block())

        def load_src(sp, T, b):
            cols = (x_cols, ctx_cols)[T]
            if isinstance(b, int) and b == 0:
                a = cols[0:1]
            else:
                a = cols[bass.ds(b, 1)]
            sp.dma_start(src[T][:, :, :], a.rearrange("b (k p) s -> p (b k) s", p=P)).then_inc(src_in[T].sem, 16)

        def load_res(sp, b):
            a = x_rows[0:1] if isinstance(b, int) and b == 0 else x_rows[bass.ds(b, 1)]
            sp.dma_start(x_res[:, :, :], a.rearrange("b (t p) d -> p (b t) d", p=P)).then_inc(res_in.sem, 16)

        @block.sync
        def _(sp):
            loads = [
                (wqk[SELF][:, :, :], w_self["qk"].rearrange("(k p) n -> p k n", p=P)),
                (src[SELF][:, :, :], None),
                (wv[SELF][:, :, :], w_self["v"].rearrange("(k p) n -> p k n", p=P)),
                (wqk[CROSS][:, :, 0:D], w_cross["q"].rearrange("(k p) n -> p k n", p=P)),
                (wqk[CROSS][:, :, D:2 * D], w_cross["k"].rearrange("(k p) n -> p k n", p=P)),
                (wv[CROSS][:, :, :], w_cross["v"].rearrange("(k p) n -> p k n", p=P)),
                (wo[:, :, :], w_cross["o"].rearrange("(k p) n -> p k n", p=P)),
                (rope_c[:, :, :], tables["cos"].rearrange("(t p) r -> p t r", p=P)),
                (rope_s[:, :, :], tables["sin"].rearrange("(t p) r -> p t r", p=P)),
                (ident[:, :], tables["ident"]),
                (mask_i[:, :], mask_cols),
                (rw[:, :, :], router["w"].rearrange("(k p) e -> p k e", p=P)),
                (rb[:, :], router["b"].partition_broadcast(P)),
                (bias_qk[:, 0:D], biases["q"].partition_broadcast(P)),
                (bias_qk[:, D:2 * D], biases["k"].partition_broadcast(P)),
                (bias_v[:, :], biases["v"].partition_broadcast(P)),
                (bias_o[:, :], biases["o"].partition_broadcast(P)),
            ]
            n = 0
            for dst, a in loads:
                if a is None:
                    load_src(sp, SELF, 0)
                else:
                    sp.dma_start(dst, a).then_inc(load_w.sem, 16)
                    n += 16
            assert n == load_w.per, n
            load_src(sp, CROSS, 0)
            load_res(sp, 0)
            sp.wait_ge(zeroed.sem, zeroed.count(0, 1))
            for part in slots.rearrange("(n p r) d -> n p (r d)", p=P, r=8):
                sp.dma_start(part, zero[:, :]).then_inc(slots_zero, 16)

            def emit(i, X, Y, bX, bY):
                if there(bX) and there(bX + 1):
                    sp.wait_ge(v_mm[X].sem, v_mm[X].count(bX))
                    sp.wait_ge(qk_mm[X].sem, qk_mm[X].count(bX))
                    load_src(sp, X, bX + 1)
                if X == SELF and there(bX - 1) and there(bX):
                    if ln[SELF].due(bX - 1, 6):
                        sp.wait_ge(ln[SELF].sem, ln[SELF].count(bX - 1, 6))
                    load_res(sp, bX)
                if X == CROSS and there(bX - 1):
                    if ln[CROSS].due(bX - 1):
                        sp.wait_ge(ln[CROSS].sem, ln[CROSS].count(bX - 1))
                    if x2_sent.due(bX - 2):
                        sp.wait_ge(x2_sent.sem, x2_sent.count(bX - 2))
                    sp.dma_start(x2_out[bass.ds(bX - 1, 1), :, :].rearrange("b (t p) d -> p (b t) d", p=P),
                                 x2[:, :, :]).then_inc(x2_sent.sem, 16)
                if there(bX):
                    sp.wait_ge(neg_ev[X].sem, neg_ev[X].count(bX))
                    if max_in[X].due(bX - 1):
                        sp.wait_ge(max_in[X].sem, max_in[X].count(bX - 1))
                    for j in range(3):
                        sp.dma_start(stack[X][MASKED + j:MASKED + j + 1, Q, :, :],
                                     nrows[j * H:(j + 1) * H, :]).then_inc(max_in[X].sem, 16)
            slots_of(emit, sp)
            sp.wait_ge(x2_sent.sem, x2_sent.count(NB - 1))
            sp.wait_ge(slots_zero, slots.shape[0] // (8 * P) * 16)

        @block.tensor
        def _(pe):
            pe.wait_ge(load_w.sem, load_w.count(0, load_w.per))
            pe.wait_ge(consts.sem, consts.count(0))
            pe.wait_ge(masks.sem, masks.count(0))
            held = {}

            def take_bank(name, T, b, k=0):
                n = bank(name, T, k)
                if n in held:
                    steps_of, at_b, at_k = held[n]
                    pe.wait_ge(steps_of.sem, steps_of.count(at_b, at_k))
                held[n] = reader(name, T, b, k)

            def values(X, b, t):
                if t == 0:
                    pe.wait_ge(src_in[X].sem, src_in[X].count(b))
                    take_bank("values", X, b)
                for k in range(KD):
                    mm = nc.tensor.matmul(work("values", X)[:, t * D:(t + 1) * D], src[X][:, k, t * P:(t + 1) * P],
                                          wv[X][:, k, :], start=(k == 0), stop=(k == KD - 1))
                if t == T2 - 1:
                    mm.then_inc(v_mm[X].sem, 1)

            def project(Y, b, n):
                half, piece = divmod(n, 2)
                if piece == 0:
                    take_bank("project", Y, b, half)
                if n == 0:
                    pe.wait_ge(src_in[Y].sem, src_in[Y].count(b))
                out = work("project", Y, half)
                if Y == SELF:
                    mm = nc.tensor.matmul(out, src[SELF][:, piece, half * P:(half + 1) * P], wqk[SELF][:, piece, :],
                                          start=(piece == 0), stop=(piece == KD - 1))
                else:
                    part, left = ((K, src[CROSS]), (Q, x1T))[half]
                    if n == 2:
                        pe.wait_ge(col_ev[SELF].sem, col_ev[SELF].count(b))
                    for k in range(KD):
                        mm = nc.tensor.matmul(out[:, piece * D:(piece + 1) * D], left[:, k, piece * P:(piece + 1) * P],
                                              wqk[CROSS][:, k, part * D:(part + 1) * D],
                                              start=(k == 0), stop=(k == KD - 1))
                if piece == 1:
                    mm.then_inc(qk_mm[Y].sem, 1)

            def make_stack(Y, b, g):
                for split in (split_p, split_a, split_v):
                    pe.wait_ge(split[Y].sem, split[Y].count(b))
                for part, name in ((Q, "stack_q"), (K, "stack_k")):
                    take_bank(name, Y, b, g)
                    columns_of = work_b(name, Y, g).rearrange("p (h s) -> p h s", h=4)
                    for j in range(4):
                        for t in range(T2):
                            mm = nc.tensor.transpose(columns_of[0:STACK, j, t * P:(t + 1) * P],
                                                     parts[Y][:, t, part, 4 * g + j, :], ident_b[:, :])
                    mm.then_inc(tr_mm[Y].sem, 1)

            def scores(X, b, h):
                if h % 4 == 0:
                    pe.wait_ge(tr_evq[X].sem, tr_evq[X].count(b, h // 4 + 1))
                    pe.wait_ge(tr_evk[X].sem, tr_evk[X].count(b, h // 4 + 1))
                if h >= 2:
                    pe.wait_ge(s_max[X].sem, s_max[X].count(b, h - 1))
                elif h == 0:
                    if s_max[1 - X].due(before(X, b)):
                        pe.wait_ge(s_max[1 - X].sem, s_max[1 - X].count(before(X, b)))
                    if s_max[X].due(b - 1):
                        pe.wait_ge(s_max[X].sem, s_max[X].count(b - 1))
                for t in range(T2):
                    mm = nc.tensor.matmul(ps_s[:, h % 2, t, :], stack[X][0:MASKED, Q, h, t * P:(t + 1) * P],
                                          stack[X][0:MASKED, K, h, :], start=True, stop=True)
                mm.then_inc(s_mm[X].sem, 1)

            def shifted(Y, b, h):
                if h == 0:
                    pe.wait_ge(max_in[Y].sem, max_in[Y].count(b))
                if h >= 2:
                    pe.wait_ge(e_exp[Y].sem, e_exp[Y].count(b, h - 1))
                elif h == 0:
                    if e_exp[1 - Y].due(before(Y, b)):
                        pe.wait_ge(e_exp[1 - Y].sem, e_exp[1 - Y].count(before(Y, b)))
                    if e_exp[Y].due(b - 1):
                        pe.wait_ge(e_exp[Y].sem, e_exp[Y].count(b - 1))
                for t in range(T2):
                    mm = nc.tensor.matmul(ps_e[:, h % 2, t, :], stack[Y][0:STACK, K, h, t * P:(t + 1) * P],
                                          stack[Y][0:STACK, Q, h, :], start=True, stop=True)
                mm.then_inc(e_mm[Y].sem, 1)

            def with_values(Y, b, h):
                pe.wait_ge(e_exp[Y].sem, e_exp[Y].count(b, h + 1))
                if h == 0:
                    pe.wait_ge(v_ev[Y].sem, v_ev[Y].count(b))
                    if pv_ev[1 - Y].due(before(Y, b)):
                        pe.wait_ge(pv_ev[1 - Y].sem, pv_ev[1 - Y].count(before(Y, b)))
                    if pv_ev[Y].due(b - 1):
                        pe.wait_ge(pv_ev[Y].sem, pv_ev[Y].count(b - 1))
                elif h % 4 == 0:
                    pe.wait_ge(pv_ev[Y].sem, pv_ev[Y].count(b, h // 4))
                q = h % 4 * 32
                for t in range(T2):
                    mm = nc.tensor.matmul(ps_o[q:q + 32, 0:S], val[Y][:, t, h, :],
                                          prob[:, h % 4, t * S:(t + 1) * S], start=(t == 0), stop=(t == T2 - 1))
                mm.then_inc(pv_mm[Y].sem, 1)

            def out_rows(X, b, t):
                pe.wait_ge(pv_ev[X].sem, pv_ev[X].count(b))
                take_bank("out_rows", X, b, t)
                for g in range(4):
                    mm = nc.tensor.transpose(work("out_rows", X, t)[:, g * P:(g + 1) * P], outT[X][:, g, t * P:(t + 1) * P], ident[:, :])
                mm.then_inc(o_mm[X].sem, 1)

            def columns(X, b):
                pe.wait_ge(ln[X].sem, ln[X].count(b, 12 if X == SELF else 4))
                take_bank("columns", X, b)
                rows = x1 if X == SELF else att2
                for k in range(KD):
                    for t in range(T2):
                        mm = nc.tensor.transpose(work("columns", X)[:, k * S + t * P:k * S + (t + 1) * P],
                                                 rows[:, t, k * P:(k + 1) * P], ident[:, :])
                mm.then_inc(col_mm[X].sem, 1)

            def project_out(b, t):
                if t == 0:
                    pe.wait_ge(col_ev[CROSS].sem, col_ev[CROSS].count(b))
                    take_bank("project_out", CROSS, b)
                for k in range(KD):
                    mm = nc.tensor.matmul(work("project_out", CROSS)[:, t * D:(t + 1) * D],
                                          attT[:, k, t * P:(t + 1) * P], wo[:, k, :], start=(k == 0), stop=(k == KD - 1))
                if t == T2 - 1:
                    mm.then_inc(proj_mm.sem, 1)

            def x2_columns(b):
                pe.wait_ge(ln[CROSS].sem, ln[CROSS].count(b))
                take_bank("x2_columns", CROSS, b)
                for k in range(KD):
                    for t in range(T2):
                        mm = nc.tensor.transpose(work("x2_columns", CROSS)[:, k * S + t * P:k * S + (t + 1) * P],
                                                 x2[:, t, k * P:(k + 1) * P], ident[:, :])
                mm.then_inc(x2T_mm.sem, 1)

            def route(b):
                pe.wait_ge(x2T_ev.sem, x2T_ev.count(b))
                take_bank("route", CROSS, b)
                for t in range(T2):
                    for k in range(KD):
                        mm = nc.tensor.matmul(work("route", CROSS)[:, t * 8:(t + 1) * 8], x2T[:, k, t * P:(t + 1) * P],
                                              rw[:, k, :], start=(k == 0), stop=(k == KD - 1))
                mm.then_inc(r_mm.sem, 1)

            def max_rows(X, b):
                pe.wait_ge(neg[X].sem, neg[X].count(b))
                take_bank("max_rows", X, b)
                pe.sem_inc(fences["pe"])
                for t in range(T2):
                    mm = nc.tensor.transpose(work_b("max_rows", X)[0:3 * H, t * P:(t + 1) * P],
                                             nparts[:, t, :, :].rearrange("p a h -> p (a h)"), ident_b[:, :])
                mm.then_inc(neg_mm[X].sem, 1)

            def emit(i, X, Y, bX, bY):
                if X == SELF and (not isinstance(i, int) or 3 <= i < NB):
                    held.update(readers_after(i - 1))
                for n in range(21):
                    if there(bX) and n < H:
                        scores(X, bX, n)
                    if there(bY) and 3 <= n < H + 3:
                        shifted(Y, bY, n - 3)
                    if there(bY) and n >= 5:
                        with_values(Y, bY, n - 5)
                    if there(bX - 1) and n in at[X]["out_rows"]:
                        out_rows(X, bX - 1, at[X]["out_rows"].index(n))
                    if there(bX) and n in at[X]["values"]:
                        values(X, bX, at[X]["values"].index(n))
                    if there(bX - 1) and n == at[X]["columns"]:
                        columns(X, bX - 1)
                    if there(bX - 1) and X == CROSS:
                        if n in at[X]["project_out"]:
                            project_out(bX - 1, at[X]["project_out"].index(n))
                        if n == at[X]["x2_columns"]:
                            x2_columns(bX - 1)
                        if n == at[X]["route"]:
                            route(bX - 1)
                    if there(bY + 1) and n in for_y[Y]["project"]:
                        project(Y, bY + 1, for_y[Y]["project"].index(n))
                    if there(bX) and n == at[X]["max_rows"]:
                        max_rows(X, bX)
                    if there(bY + 1) and n in for_y[Y]["stack"]:
                        make_stack(Y, bY + 1, for_y[Y]["stack"].index(n))

            for n in range(4):
                project(SELF, 0, n)
            for g in range(4):
                make_stack(SELF, 0, g)
            slots_of(emit, pe)

        @block.scalar
        def _(act):
            def stack_q(Y, b, g):
                act.wait_ge(tr_mm[Y].sem, tr_mm[Y].count(b, 2 * g + 1))
                if e_mm[Y].due(b - 1, 4 * g + 4):
                    act.wait_ge(e_mm[Y].sem, e_mm[Y].count(b - 1, 4 * g + 4))
                nc.scalar.copy(stack[Y][0:STACK, Q, 4 * g:4 * g + 4, :],
                               work_b("stack_q", Y, g)[0:STACK].rearrange("p (h s) -> p h s", h=4)).then_inc(tr_evq[Y].sem, 1)

            def split_steps(Y, b, n):
                if n == 0 and tr_mm[Y].due(b - 1):
                    act.wait_ge(tr_mm[Y].sem, tr_mm[Y].count(b - 1))
                if n == 0 and Y == CROSS:
                    act.wait_ge(qk_ev[Y].sem, qk_ev[Y].count(b))
                if n == 2:
                    for t in range(T2):
                        put_parts(nc.scalar.copy, Y, t, Q, 0, qk[Y]).then_inc(split_a[Y].sem, 1)
                    return
                slot, t = (0, n) if n < 2 else (1, n - 3)
                act.wait_ge(split_p[Y].sem, split_p[Y].count(b, split_p[Y].per - 6 + 2 * slot + t + 1))
                nc.scalar.copy(parts[Y][:, t, :, :, slot * R:(slot + 1) * R],
                               by_head((qk[Y], rest)[slot], t)).then_inc(split_a[Y].sem, 1)

            def exponentials(Y, b, h):
                act.wait_ge(e_mm[Y].sem, e_mm[Y].count(b, h + 1))
                if h >= 4:
                    act.wait_ge(pv_mm[Y].sem, pv_mm[Y].count(b, h - 3))
                elif h == 0:
                    if pv_mm[1 - Y].due(before(Y, b)):
                        act.wait_ge(pv_mm[1 - Y].sem, pv_mm[1 - Y].count(before(Y, b)))
                    if pv_mm[Y].due(b - 1):
                        act.wait_ge(pv_mm[Y].sem, pv_mm[Y].count(b - 1))
                nc.scalar.activation(prob[:, h % 4, :], ps_e[:, h % 2, :, :].rearrange("p t s -> p (t s)"),
                                     ACT.Exp, scale=SCALE).then_inc(e_exp[Y].sem, 1)

            def out_columns(Y, b, g):
                act.wait_ge(pv_mm[Y].sem, pv_mm[Y].count(b, 4 * g + 4))
                if g == 0:
                    if o_mm[Y].due(b - 1):
                        act.wait_ge(o_mm[Y].sem, o_mm[Y].count(b - 1))
                nc.scalar.copy(outT[Y][:, g, :], ps_o[:, 0:S]).then_inc(pv_ev[Y].sem, 1)

            def columns(X, b):
                act.wait_ge(col_mm[X].sem, col_mm[X].count(b))
                if X == SELF:
                    if qk_mm[CROSS].due(b - 1):
                        act.wait_ge(qk_mm[CROSS].sem, qk_mm[CROSS].count(b - 1))
                else:
                    if proj_mm.due(b - 1):
                        act.wait_ge(proj_mm.sem, proj_mm.count(b - 1))
                nc.scalar.copy((x1T if X == SELF else attT)[:, :, :],
                               work("columns", X).rearrange("p (k s) -> p k s", k=KD)).then_inc(col_ev[X].sem, 1)

            def x2_columns(b):
                act.wait_ge(x2T_mm.sem, x2T_mm.count(b))
                if r_mm.due(b - 1):
                    act.wait_ge(r_mm.sem, r_mm.count(b - 1))
                nc.scalar.copy(x2T[:, :, :], work("x2_columns", CROSS).rearrange("p (k s) -> p k s", k=KD)).then_inc(x2T_ev.sem, 1)

            def emit(i, X, Y, bX, bY):
                for n in range(21):
                    if there(bY) and 3 <= n < H + 3:
                        exponentials(Y, bY, n - 3)
                    if there(bY) and n >= 5 and (n - 5) % 4 == 3:
                        out_columns(Y, bY, (n - 5) // 4)
                    if there(bX - 1) and n == at[X]["columns"]:
                        columns(X, bX - 1)
                    if there(bX - 1) and X == CROSS and n == at[X]["x2_columns"]:
                        x2_columns(bX - 1)
                    if there(bY + 1) and n in for_y[Y]["split_a"]:
                        split_steps(Y, bY + 1, for_y[Y]["split_a"].index(n))
                    if there(bY + 1) and n in for_y[Y]["stack"]:
                        stack_q(Y, bY + 1, for_y[Y]["stack"].index(n))

            for n in range(5):
                split_steps(SELF, 0, n)
            for g in range(4):
                stack_q(SELF, 0, g)
            slots_of(emit, act)

        @block.vector
        def _(dve):
            nc.vector.memset(zero[:, :], 0.0).then_inc(zeroed.sem, 1)
            for T in (SELF, CROSS):
                nc.vector.memset(val[T][:, :, :, :], 1.0).then_inc(consts.sem, 1)
                nc.vector.memset(parts[T][:, :, :, :, :], 0.0).then_inc(consts.sem, 1)
                dve.wait_ge(consts.sem, consts.count(0, 3 * T + 2))
                for t in range(T2):
                    nc.vector.memset(parts[T][:, t, Q, :, DATA:MASKED], 1.0)
                    last = nc.vector.memset(parts[T][:, t, K, :, MASKED:STACK], 1.0)
                last.then_inc(consts.sem, 1)
            dve.wait_ge(load_w.sem, load_w.count(0, load_w.per))
            nc.vector.tensor_copy(ident_b[:, :], ident[:, :]).then_inc(consts.sem, 1)
            nc.vector.memset(minus_half[:, :], -0.5).then_inc(consts.sem, 1)
            nc.vector.tensor_copy(mask_f[:, :], mask_i[:, :]).then_inc(masks.sem, 1)
            dve.wait_ge(masks.sem, masks.count(0, 1))
            nc.vector.tensor_scalar(hidden_f[:, :], mask_f[:, :], 0.0, None, ALU.is_equal).then_inc(masks.sem, 1)
            dve.wait_ge(masks.sem, masks.count(0, 2))
            by_tile = hidden_f[:, :].rearrange("p (b t) -> p b t", t=T2)
            nc.vector.tensor_scalar(mask_all[:, :, :, 0], by_tile, -1.0, 1.0, ALU.mult, ALU.add).then_inc(masks.sem, 1)
            for j, part in enumerate(bf16_parts(MASK_VALUE)):
                nc.vector.tensor_scalar(mask_all[:, :, :, 1 + j], by_tile, part, None, ALU.mult).then_inc(masks.sem, 1)

            dve.wait_ge(consts.sem, consts.count(0))

            def maxima(X, b, h):
                dve.wait_ge(s_mm[X].sem, s_mm[X].count(b, h + 1))
                if h == 0:
                    if neg[X].due(b - 1):
                        dve.wait_ge(neg[X].sem, neg[X].count(b - 1))
                    if neg[1 - X].due(before(X, b)):
                        dve.wait_ge(neg[1 - X].sem, neg[1 - X].count(before(X, b)))
                nc.vector.tensor_reduce(smax[:, :, h], ps_s[:, h % 2, :, :], AX.X, ALU.max).then_inc(s_max[X].sem, 1)

            def values(X, b):
                dve.wait_ge(v_mm[X].sem, v_mm[X].count(b))
                if pv_mm[X].due(b - 1):
                    dve.wait_ge(pv_mm[X].sem, pv_mm[X].count(b - 1))
                rows = work("values", X).rearrange("p (t h r) -> p t h r", t=T2, h=H)
                if X == SELF:
                    nc.vector.tensor_copy(val[X][:, :, :, 0:R], rows).then_inc(v_ev[X].sem, 1)
                else:
                    bias = bias_v[:, :].rearrange("p (h r) -> p h r", h=H).unsqueeze(1).to_broadcast([P, T2, H, R])
                    nc.vector.tensor_tensor(val[X][:, :, :, 0:R], rows, bias, ALU.add).then_inc(v_ev[X].sem, 1)

            def queries_keys(Y, b, t):
                dve.wait_ge(qk_mm[Y].sem, qk_mm[Y].count(b, t + 1))
                if split_p[Y].due(b - 1):
                    for split in (split_p, split_a, split_v):
                        dve.wait_ge(split[Y].sem, split[Y].count(b - 1))
                if Y == CROSS:
                    part = (K, Q)[t]
                    nc.vector.tensor_tensor(qk[Y][:, :, part * D:(part + 1) * D],
                                            work("project", Y, t).rearrange("p (t d) -> p t d", t=T2),
                                            bias_qk[:, part * D:(part + 1) * D].unsqueeze(1)
                                            .to_broadcast([P, T2, D]), ALU.add)\
                      .then_inc(qk_ev[Y].sem, 1)
                    return
                pairs = work("project", Y, t).rearrange("p (h c r) -> p h c r", c=2, r=R // 2)
                cos = rope_c[:, t, :].unsqueeze(1).to_broadcast([P, 2 * 2 * H, R // 2])
                sin = rope_s[:, t, :].unsqueeze(1).to_broadcast([P, 2 * H, R // 2])
                nc.vector.tensor_tensor(qk[Y][:, t, :].rearrange("p (m r) -> p m r", r=R // 2),
                                        work("project", Y, t).rearrange("p (m r) -> p m r", r=R // 2), cos, ALU.mult)\
                  .then_inc(qk_ev[Y].sem, 1)
                turned = rot[:, t, :].rearrange("p (h c r) -> p h c r", c=2, r=R // 2)
                nc.vector.scalar_tensor_tensor(turned[:, :, 0, :], pairs[:, :, 1, :], -1.0, sin, ALU.mult, ALU.mult)\
                  .then_inc(qk_ev[Y].sem, 1)
                nc.vector.tensor_tensor(turned[:, :, 1, :], pairs[:, :, 0, :], sin, ALU.mult).then_inc(qk_ev[Y].sem, 1)

            def split_steps(Y, b, n):
                if n == 0 and tr_mm[Y].due(b - 1):
                    dve.wait_ge(tr_mm[Y].sem, tr_mm[Y].count(b - 1))
                level, t = divmod(n, T2)
                dve.wait_ge(split_p[Y].sem, split_p[Y].count(b, split_p[Y].per - 6 + n + 1))
                for part in (K,) if level == 0 else (Q, K):
                    put_parts(nc.vector.tensor_copy, Y, t, part, level, (qk[Y], rest, rest2)[level])\
                      .then_inc(split_v[Y].sem, 1)

            def stack_k(Y, b, g):
                dve.wait_ge(tr_mm[Y].sem, tr_mm[Y].count(b, 2 * g + 2))
                if e_mm[Y].due(b - 1, 4 * g + 4):
                    dve.wait_ge(e_mm[Y].sem, e_mm[Y].count(b - 1, 4 * g + 4))
                nc.vector.tensor_copy(stack[Y][0:STACK, K, 4 * g:4 * g + 4, :],
                                      work_b("stack_k", Y, g)[0:STACK].rearrange("p (h s) -> p h s", h=4)).then_inc(tr_evk[Y].sem, 1)

            def max_rows(X, b):
                dve.wait_ge(neg_mm[X].sem, neg_mm[X].count(b))
                if max_in[1 - X].due(before(X, b)):
                    dve.wait_ge(max_in[1 - X].sem, max_in[1 - X].count(before(X, b)))
                if max_in[X].due(b - 1):
                    dve.wait_ge(max_in[X].sem, max_in[X].count(b - 1))
                nc.vector.tensor_copy(nrows[:, :], work_b("max_rows", X)[0:3 * H, 0:S]).then_inc(neg_ev[X].sem, 1)

            def mean_and_variance(X, b, done, rows, st):
                s = ln[X]
                dve.wait_ge(s.sem, s.count(b, done))
                for t in range(T2):
                    nc.vector.bn_stats(st[:, t, :], rows[:, t, :]).then_inc(s.sem, 1)
                dve.wait_ge(s.sem, s.count(b, done + 2))
                dve.sem_inc(fences["dve"])
                for t in range(T2):
                    nc.vector.bn_aggr(mv[X][:, t, :], st[:, t, :]).then_inc(s.sem, 1)

            def normalise(X, b, rows, out):
                s = ln[X]
                dve.wait_ge(ln_r[X].sem, ln_r[X].count(b))
                for t in range(T2):
                    nc.vector.tensor_scalar(out[:, t, :], rows[:, t, :], mv[X][:, t, 0:1], rstd[X][:, t:t + 1],
                                            ALU.subtract, ALU.mult).then_inc(s.sem, 1)

            def divide(X, b, t):
                s, dst = ln[X], (att, att2)[X]
                dve.wait_ge(o_mm[X].sem, o_mm[X].count(b, t + 1))
                heads = work("out_rows", X, t).rearrange("p (h r) -> p h r", h=H)
                if t == 0:
                    if col_mm[X].due(b - 1):
                        dve.wait_ge(col_mm[X].sem, col_mm[X].count(b - 1))
                    if s.due(b - 1):
                        dve.wait_ge(s.sem, s.count(b - 1))
                    if ln[1 - X].due(before(X, b)):
                        dve.wait_ge(ln[1 - X].sem, ln[1 - X].count(before(X, b)))
                nc.vector.reciprocal(rden[:, t, :], heads[:, :, R]).then_inc(s.sem, 1)
                dve.wait_ge(s.sem, s.count(b, 2 * t + 1))
                nc.vector.tensor_tensor(dst[:, t, :].rearrange("p (h r) -> p h r", h=H), heads[:, :, 0:R],
                                        rden[:, t, :].unsqueeze(2).to_broadcast([P, H, R]), ALU.mult)\
                  .then_inc(s.sem, 1)

            def first_norm(b):
                dve.wait_ge(res_in.sem, res_in.count(b))
                dve.wait_ge(ln[SELF].sem, ln[SELF].count(b, 4))
                for t in range(T2):
                    nc.vector.tensor_tensor(y[:, t, :], att[:, t, :], x_res[:, t, :], ALU.add).then_inc(ln[SELF].sem, 1)
                mean_and_variance(SELF, b, 6, y, stats)

            def first_normed(b):
                if col_mm[SELF].due(b - 1):
                    dve.wait_ge(col_mm[SELF].sem, col_mm[SELF].count(b - 1))
                if x1b_made.due(b - 1):
                    dve.wait_ge(x1b_made.sem, x1b_made.count(b - 1))
                normalise(SELF, b, y, x1)

            def second_norm(b):
                dve.wait_ge(proj_mm.sem, proj_mm.count(b))
                dve.wait_ge(x1b_made.sem, x1b_made.count(b))
                nc.vector.tensor_tensor(y2[:, :, :].rearrange("p t d -> p (t d)"), work("project_out", CROSS),
                                        x1b[:, :, :].rearrange("p t d -> p (t d)"), ALU.add).then_inc(ln[CROSS].sem, 1)
                mean_and_variance(CROSS, b, 5, y2, stats2)

            def second_normed(b):
                if x2_sent.due(b - 1):
                    dve.wait_ge(x2_sent.sem, x2_sent.count(b - 1))
                if x2T_mm.due(b - 1):
                    dve.wait_ge(x2T_mm.sem, x2T_mm.count(b - 1))
                normalise(CROSS, b, y2, x2)

            def routing_logits(b):
                dve.wait_ge(r_mm.sem, r_mm.count(b))
                nc.vector.tensor_tensor(logits[:, bass.ds(b, 1), :, :].rearrange("p b t e -> p (b t) e"),
                                        work("route", CROSS)[:, 0:T2 * 8].rearrange("p (t e) -> p t e", e=8),
                                        rb[:, :].unsqueeze(1).to_broadcast([P, T2, 8]), ALU.add).then_inc(r_ev.sem, 1)

            def emit(i, X, Y, bX, bY):
                for n in range(21):
                    if there(bX) and n < H:
                        maxima(X, bX, n)
                    if there(bX - 1) and n in at[X]["out_rows"]:
                        divide(X, bX - 1, at[X]["out_rows"].index(n))
                    if there(bX) and n == at[X]["values"][-1]:
                        values(X, bX)
                    if there(bX - 1) and n == at[X]["norm"]:
                        (first_norm, second_norm)[X](bX - 1)
                    if there(bX - 1) and n == at[X]["normed"]:
                        (first_normed, second_normed)[X](bX - 1)
                    if there(bX - 1) and X == CROSS and n == at[X]["route"]:
                        routing_logits(bX - 1)
                    if there(bY + 1) and n in for_y[Y]["project"][1::2]:
                        queries_keys(Y, bY + 1, for_y[Y]["project"].index(n) // 2)
                    if there(bY + 1) and n in for_y[Y]["split_v"]:
                        split_steps(Y, bY + 1, for_y[Y]["split_v"].index(n))
                    if there(bX) and n == at[X]["max_rows"]:
                        max_rows(X, bX)
                    if there(bY + 1) and n in for_y[Y]["stack"]:
                        stack_k(Y, bY + 1, for_y[Y]["stack"].index(n))

            queries_keys(SELF, 0, 0)
            queries_keys(SELF, 0, 1)
            for n in range(6):
                split_steps(SELF, 0, n)
            for g in range(4):
                stack_k(SELF, 0, g)
            slots_of(emit, dve)

        @block.gpsimd
        def _(pool):
            def ready():
                pool.sem_inc(fences["pool"])

            def wholes_and_rests(Y, b, between):
                tally = Tally()
                if tr_mm[Y].due(b - 1):
                    pool.wait_ge(tr_mm[Y].sem, tr_mm[Y].count(b - 1))
                if Y == CROSS:
                    ready()
                    nc.gpsimd.tensor_copy(mask_now[:, :, :], mask_all[:, bass.ds(b, 1), :, :]
                                          .rearrange("p b t m -> p (b t) m")).then_inc(split_p[Y].sem, 1)
                    pool.wait_ge(split_p[Y].sem, split_p[Y].count(b, tally.one()))
                    ready()
                    for t in range(T2):
                        nc.gpsimd.tensor_copy(parts[Y][:, t, K, :, DATA:MASKED],
                                              mask_now[:, t, 1:4].unsqueeze(1).to_broadcast([P, H, 3]))\
                          .then_inc(split_p[Y].sem, 1)
                        tally.one()
                for t in range(T2):
                    pool.wait_ge(qk_ev[Y].sem, qk_ev[Y].count(b, 3 * (t + 1) if Y == SELF else 1))
                    ready()
                    if Y == SELF:
                        nc.gpsimd.tensor_tensor(qk[Y][:, t, :], qk[Y][:, t, :], rot[:, t, :], ALU.add)\
                          .then_inc(split_p[Y].sem, 1)
                    else:
                        nc.gpsimd.tensor_scalar(qk[Y][:, t, D:2 * D], qk[Y][:, t, D:2 * D], mask_now[:, t, 0:1],
                                                None, ALU.mult).then_inc(split_p[Y].sem, 1)
                    tally.one()
                if split_v[1 - Y].due(before(Y, b)):
                    pool.wait_ge(split_v[1 - Y].sem, split_v[1 - Y].count(before(Y, b)))
                    pool.wait_ge(split_a[1 - Y].sem, split_a[1 - Y].count(before(Y, b)))
                for n, (level, left) in enumerate(((qk[Y], rest), (rest, rest2))):
                    if n == 1:
                        between()
                    for t in range(T2):
                        pool.wait_ge(split_a[Y].sem, split_a[Y].count(b, 4 * n + t + 1))
                        pool.wait_ge(split_p[Y].sem, split_p[Y].count(b, tally.n - 1))
                        ready()
                        nc.gpsimd.tensor_tensor(by_head(left, t), by_head(level, t),
                                                parts[Y][:, t, :, :, n * R:(n + 1) * R], ALU.subtract)\
                          .then_inc(split_p[Y].sem, 1)
                        tally.one()
                assert tally.n == split_p[Y].per

            def negated_maxima(X, b):
                s = neg[X]
                pool.wait_ge(s_max[X].sem, s_max[X].count(b))
                if neg_mm[X].due(b - 1):
                    pool.wait_ge(neg_mm[X].sem, neg_mm[X].count(b - 1))
                if neg_mm[1 - X].due(before(X, b)):
                    pool.wait_ge(neg_mm[1 - X].sem, neg_mm[1 - X].count(before(X, b)))
                if neg[1 - X].due(before(X, b)):
                    pool.wait_ge(neg[1 - X].sem, neg[1 - X].count(before(X, b)))
                if neg[X].due(b - 1):
                    pool.wait_ge(neg[X].sem, neg[X].count(b - 1))
                ready()
                nc.gpsimd.tensor_scalar(nmax[:, :, :], smax[:, :, :], -1.0, None, ALU.mult).then_inc(s.sem, 1)
                level = nmax
                for j in range(3):
                    pool.wait_ge(s.sem, s.count(b, 1 + 2 * j))
                    ready()
                    nc.gpsimd.tensor_copy(nparts[:, :, j, :], level[:, :, :]).then_inc(s.sem, 1)
                    if j < 2:
                        pool.wait_ge(s.sem, s.count(b, 2 + 2 * j))
                        ready()
                        new = (nrest, nrest2)[j]
                        nc.gpsimd.tensor_tensor(new[:, :, :], level[:, :, :], nparts[:, :, j, :], ALU.subtract)\
                          .then_inc(s.sem, 1)
                        level = new

            def inverse_deviation(X, b):
                pool.wait_ge(ln[X].sem, ln[X].count(b, 10 if X == SELF else 9))
                ready()
                nc.gpsimd.tensor_scalar(veps[X][:, :], mv[X][:, :, 1], EPS, None, ALU.add).then_inc(ln_r[X].sem, 1)
                pool.wait_ge(ln_r[X].sem, ln_r[X].count(b, 1))
                ready()
                nc.gpsimd.tensor_tensor(rstd[X][:, :], veps[X][:, :], minus_half[:, :], ALU.pow).then_inc(ln_r[X].sem, 1)

            def residual_with_bias(b):
                pool.wait_ge(ln[SELF].sem, ln[SELF].count(b))
                if ln[CROSS].due(b - 1, 5):
                    pool.wait_ge(ln[CROSS].sem, ln[CROSS].count(b - 1, 5))
                ready()
                nc.gpsimd.tensor_tensor(x1b[:, :, :], x1[:, :, :], bias_o[:, :].unsqueeze(1).to_broadcast([P, T2, D]),
                                        ALU.add).then_inc(x1b_made.sem, 1)

            def emit(i, X, Y, bX, bY):
                def invert():
                    if there(bX - 1):
                        inverse_deviation(X, bX - 1)

                if X == SELF:
                    invert()
                if there(bY + 1):
                    wholes_and_rests(Y, bY + 1, (lambda: None) if X == SELF else invert)
                elif X == CROSS:
                    invert()
                if X == CROSS and there(bX):
                    residual_with_bias(bX)
                if there(bX):
                    negated_maxima(X, bX)

            pool.wait_ge(load_w.sem, load_w.count(0, load_w.per))
            pool.wait_ge(consts.sem, consts.count(0))
            pool.wait_ge(masks.sem, masks.count(0))
            ready()
            wholes_and_rests(SELF, 0, lambda: None)
            slots_of(emit, pool)


E = 8
F = 1024
TOP = 2
TILES = 32 * T2
CAP = -(-32 * S * 5 // (E * 4))
ROWS = E * CAP
SKIP = 4 * ROWS
CT = 5
CHUNK = CT * P
CHUNKS = ROWS // CHUNK
HALF = CHUNK // 2
FT = F // P
GT = 4
GROUPS = TILES // GT


CHOSEN = 6 + 5 + 1 + 5 + 4


def routing(nc, logits, tables, slot_s, slot_g, weight):
    ctx = ExitStack()
    with ctx:
        def sb(name, shape, dt=F32):
            return ctx.enter_context(nc.sbuf_tensor(name, shape, dt))

        def sem(name):
            return ctx.enter_context(nc.semaphore(name))

        rank = sb("rank", [P, E])
        first_slot = sb("first_slot", [P, E])
        upto = sb("upto", [P, P], BF16)
        upto_f = sb("upto_f", [P, P])
        ones_b = sb("ones_b", [P, P], BF16)
        ones = sb("ones_t", [P, TILES])
        top = sb("top", [P, TILES])
        gates = sb("gates", [P, TILES, E])
        left = sb("left", [P, TILES, E])
        hit = sb("hit", [P, TILES, E])
        pick = [sb(f"pick{c}", [P, TILES, E]) for c in range(TOP)]
        chosen = sb("chosen", [P, TILES, E], BF16)
        total = sb("total", [P, TILES, E])
        running = sb("running", [P, TILES, E])
        pos = sb("pos", [P, TILES, E])
        valid = sb("valid", [P, TILES, E])
        work = sb("work", [P, TILES, E])
        slot_f = sb("slot_f", [P, TILES])
        valid_f = sb("valid_f", [P, TILES])
        tmp = sb("tmp", [P, TILES])
        ps_within = ctx.enter_context(nc.psum_tensor("ps_within", [P, TILES * E], F32))
        ps_total = ctx.enter_context(nc.psum_tensor("ps_total", [P, TILES * E], F32))
        loaded, step, exp_done, counted = sem("r_loaded"), sem("r_step"), sem("r_exp"), sem("r_counted")
        block = ctx.enter_context(nc.Block())

        @block.sync
        def _(sp):
            sp.dma_start(rank[:, :], tables["rank"].partition_broadcast(P)).then_inc(loaded, 16)
            sp.dma_start(first_slot[:, :], tables["first_slot"].partition_broadcast(P)).then_inc(loaded, 16)
            sp.dma_start(upto_f[:, :], tables["upto"]).then_inc(loaded, 16)

        @block.scalar
        def _(act):
            act.wait_ge(step, 2)
            nc.scalar.activation(gates[:, :, :], left[:, :, :], ACT.Exp).then_inc(exp_done, 1)

        @block.tensor
        def _(pe):
            pe.wait_ge(step, CHOSEN)
            nc.tensor.matmul(ps_within[:, :], upto[:, :], chosen[:, :, :].rearrange("p t e -> p (t e)"),
                             start=True, stop=True)
            nc.tensor.matmul(ps_total[:, :], ones_b[:, :], chosen[:, :, :].rearrange("p t e -> p (t e)"),
                             start=True, stop=True).then_inc(counted, 1)

        @block.vector
        def _(dve):
            tally = Tally()

            def wide(a):
                return a.unsqueeze(2).to_broadcast([P, TILES, E])

            def by_expert(a):
                return a.unsqueeze(1).to_broadcast([P, TILES, E])

            v = nc.vector
            lg = logits[:, :, :, :].rearrange("p b t e -> p (b t) e")
            v.tensor_reduce(top[:, :], lg, AX.X, ALU.max).then_inc(step, 1)
            dve.wait_ge(step, tally.one())
            v.tensor_tensor(left[:, :, :], lg, wide(top[:, :]), ALU.subtract).then_inc(step, 1)
            dve.wait_ge(step, tally.one())
            dve.wait_ge(exp_done, 1)
            v.tensor_reduce(top[:, :], gates[:, :, :], AX.X, ALU.add).then_inc(step, 1)
            dve.wait_ge(step, tally.one())
            v.reciprocal(tmp[:, :], top[:, :]).then_inc(step, 1)
            dve.wait_ge(step, tally.one())
            v.tensor_tensor(gates[:, :, :], gates[:, :, :], wide(tmp[:, :]), ALU.mult).then_inc(step, 1)
            dve.wait_ge(step, tally.one())
            v.tensor_copy(left[:, :, :], gates[:, :, :]).then_inc(step, 1)
            dve.wait_ge(step, tally.one())
            dve.wait_ge(loaded, 48)
            for c in range(TOP):
                v.tensor_reduce(top[:, :], left[:, :, :], AX.X, ALU.max).then_inc(step, 1)
                dve.wait_ge(step, tally.one())
                v.tensor_tensor(hit[:, :, :], left[:, :, :], wide(top[:, :]), ALU.is_equal).then_inc(step, 1)
                dve.wait_ge(step, tally.one())
                v.tensor_tensor(hit[:, :, :], hit[:, :, :], by_expert(rank[:, :]), ALU.mult).then_inc(step, 1)
                dve.wait_ge(step, tally.one())
                v.tensor_reduce(top[:, :], hit[:, :, :], AX.X, ALU.max).then_inc(step, 1)
                dve.wait_ge(step, tally.one())
                v.tensor_tensor(pick[c][:, :, :], hit[:, :, :], wide(top[:, :]), ALU.is_equal).then_inc(step, 1)
                dve.wait_ge(step, tally.one())
                if c == 0:
                    v.scalar_tensor_tensor(left[:, :, :], pick[0][:, :, :], -2.0, left[:, :, :], ALU.mult, ALU.add).then_inc(step, 1)
                    dve.wait_ge(step, tally.one())
            v.memset(ones_b[:, :], 1.0).then_inc(step, 1)
            dve.wait_ge(step, tally.one())
            v.memset(ones[:, :], 1.0).then_inc(step, 1)
            dve.wait_ge(step, tally.one())
            v.tensor_copy(upto[:, :], upto_f[:, :]).then_inc(step, 1)
            dve.wait_ge(step, tally.one())
            v.tensor_tensor(chosen[:, :, :], pick[0][:, :, :], pick[1][:, :, :], ALU.add).then_inc(step, 1)
            dve.wait_ge(step, tally.one())
            assert tally.n == CHOSEN
            dve.wait_ge(counted, 1)
            v.tensor_copy(total[:, :, :].rearrange("p t e -> p (t e)"), ps_total[:, :]).then_inc(step, 1)
            dve.wait_ge(step, tally.one())
            for e in range(E):
                v.tensor_tensor_scan(running[:, :, e], ones[:, :], total[:, :, e], 0.0, ALU.mult, ALU.add).then_inc(step, 1)
                dve.wait_ge(step, tally.one())
            v.tensor_tensor(running[:, :, :], running[:, :, :], total[:, :, :], ALU.subtract).then_inc(step, 1)
            dve.wait_ge(step, tally.one())
            v.scalar_tensor_tensor(pos[:, :, :].rearrange("p t e -> p (t e)"), ps_within[:, :], -1.0,
                                      running[:, :, :].rearrange("p t e -> p (t e)"), ALU.add, ALU.add).then_inc(step, 1)
            dve.wait_ge(step, tally.one())
            v.scalar_tensor_tensor(valid[:, :, :], pos[:, :, :], float(CAP), chosen[:, :, :], ALU.is_lt, ALU.mult).then_inc(step, 1)
            dve.wait_ge(step, tally.one())
            v.tensor_tensor(pos[:, :, :], pos[:, :, :], by_expert(first_slot[:, :]), ALU.add).then_inc(step, 1)
            dve.wait_ge(step, tally.one())
            v.tensor_tensor(gates[:, :, :], gates[:, :, :], valid[:, :, :], ALU.mult).then_inc(step, 1)
            dve.wait_ge(step, tally.one())
            for c in range(TOP):
                for src, dst in ((pos, slot_f[:, :]), (valid, valid_f[:, :]), (gates, weight[:, c, :])):
                    v.tensor_tensor(work[:, :, :], pick[c][:, :, :], src[:, :, :], ALU.mult).then_inc(step, 1)
                    dve.wait_ge(step, tally.one())
                    v.tensor_reduce(dst, work[:, :, :], AX.X, ALU.add).then_inc(step, 1)
                    dve.wait_ge(step, tally.one())
                v.tensor_tensor(slot_f[:, :], slot_f[:, :], valid_f[:, :], ALU.mult).then_inc(step, 1)
                dve.wait_ge(step, tally.one())
                v.tensor_copy(slot_g[:, c, :], slot_f[:, :]).then_inc(step, 1)
                dve.wait_ge(step, tally.one())
                v.tensor_scalar(tmp[:, :], valid_f[:, :], -float(SKIP), float(SKIP), ALU.mult, ALU.add).then_inc(step, 1)
                dve.wait_ge(step, tally.one())
                v.tensor_tensor(slot_f[:, :], slot_f[:, :], tmp[:, :], ALU.add).then_inc(step, 1)
                dve.wait_ge(step, tally.one())
                v.tensor_copy(slot_s[:, c, :], slot_f[:, :]).then_inc(step, 1)
                dve.wait_ge(step, tally.one())


def in_pairs(eng, n, emit):
    emit(0, 0)
    emit(1, 1)
    with eng.Fori(1, n // 2 - 1) as i:
        emit(i * 2, 0)
        emit(i * 2 + 1, 1)
    emit(n - 2, 0)
    emit(n - 1, 1)


class Turns:

    def __init__(self, sems, per):
        self.sems, self.per = sems, per

    def count(self, q, parity):
        return q * (self.per // 2) + (self.per - parity * (self.per // 2))

    def due(self, q):
        return not isinstance(q, int) or q >= 0


def dispatch(nc, x2_dram, slots, slot_s):
    with ExitStack() as ctx:
        rows = ctx.enter_context(nc.sbuf_tensor("d_rows", [P, 2, GT, D], F32))
        index = ctx.enter_context(nc.sbuf_tensor("d_index", [P, 2, TOP, GT], U32))

        def sem(name):
            return ctx.enter_context(nc.semaphore(name))

        come = Turns([sem("d_come0"), sem("d_come1")], 16)
        gone = Turns([sem("d_gone0"), sem("d_gone1")], 16 * TOP * GT)
        staged = Steps(sem("d_staged"), 1)
        fence = sem("d_fence")
        block = ctx.enter_context(nc.Block())

        @block.sync
        def _(sp):
            def load(q, u):
                if gone.due(q - 2):
                    sp.wait_ge(gone.sems[u], gone.count(q - 2, u))
                sp.dma_start(rows[:, u, :, :], x2_dram[bass.ds(q * (GT * P), GT * P), :]
                             .rearrange("(g p) d -> p g d", p=P)).then_inc(come.sems[u], 16)
            in_pairs(sp, GROUPS, load)

        @block.vector
        def _(dve):
            def stage(q, u):
                if gone.due(q - 2):
                    dve.wait_ge(gone.sems[u], gone.count(q - 2, u))
                nc.vector.tensor_copy(index[:, u, :, :], slot_s[:, :, bass.ds(q * GT, GT)]).then_inc(staged.sem, 1)
            in_pairs(dve, GROUPS, stage)

        @block.gpsimd
        def _(pool):
            def scatter(q, u):
                pool.wait_ge(staged.sem, staged.count(q))
                pool.wait_ge(come.sems[u], come.count(q, u))
                pool.sem_inc(fence)
                for g in range(GT):
                    for c in range(TOP):
                        nc.gpsimd.indirect_dma_start(
                            out=slots[:, :], out_offset=bass.IndirectOffsetOnAxis(ap=index[:, u, c, g:g + 1], axis=0),
                            in_=rows[:, u, g, :], in_offset=None, bounds_check=ROWS - 1, oob_is_err=False,
                        ).then_inc(gone.sems[u], 16)
            in_pairs(pool, GROUPS, scatter)
            for u in range(2):
                pool.wait_ge(gone.sems[u], gone.count(GROUPS - 2 + u, u))


def experts(nc, slots, results, ident_dram, w1, b1, w2, b2):
    per_expert = CAP // CHUNK
    with ExitStack() as ctx:
        def sb(name, shape, dt=F32):
            return ctx.enter_context(nc.sbuf_tensor(name, shape, dt))

        def sem(name):
            return ctx.enter_context(nc.semaphore(name))

        ident = sb("m_ident", [P, P])
        w1_sb = sb("w1_sb", [P, 2, KD, F])
        w2_sb = sb("w2_sb", [P, 2, FT, D])
        b1_sb = sb("b1_sb", [P, 2, FT])
        b2_sb = sb("b2_sb", [P, 2, D])
        rows = sb("m_rows", [P, 2, CT, D])
        cols = sb("m_cols", [P, 2, KD, CHUNK])
        hid = sb("hid", [P, FT, CHUNK])
        res = sb("m_res", [P, 2, CT, D])
        ps_t = ctx.enter_context(nc.psum_tensor("m_ps_t", [P, 2, 512], F32))
        ps_h = ctx.enter_context(nc.psum_tensor("m_ps_h", [P, 4, 512], F32))
        ps_o = ctx.enter_context(nc.psum_tensor("m_ps_o", [P, 2, 512], F32))

        id_in = sem("m_id")
        w_in = Turns([sem("w_in0"), sem("w_in1")], 64)
        rows_in = Turns([sem("m_rows_in0"), sem("m_rows_in1")], 16)
        sent = Turns([sem("m_sent0"), sem("m_sent1")], 16)
        t_mm = Steps(sem("m_t_mm"), CT)
        t_ev = Steps(sem("m_t_ev"), CT)
        h_mm = Steps(sem("m_h_mm"), 2 * FT)
        h_ev = Steps(sem("m_h_ev"), 2 * FT)
        o_mm = Steps(sem("m_o_mm"), CT)
        o_ev = Steps(sem("m_o_ev"), CT)
        fence = sem("m_fence")
        block = ctx.enter_context(nc.Block())

        def turns(eng, emit):
            def four(i):
                for u in range(4):
                    emit(i * 4 + u, i * 2 + u // per_expert, u % 2, u // per_expert)
            four(0)
            with eng.Fori(1, CHUNKS // 4 - 1) as i:
                four(i)
            four(CHUNKS // 4 - 1)

        @block.sync
        def _(sp):
            sp.dma_start(ident[:, :], ident_dram).then_inc(id_in, 16)

            def load(q, e, u, pe_):
                if u == 0:
                    if o_ev.due(q - 3):
                        sp.wait_ge(o_ev.sem, o_ev.count(q - 3))
                    for dst, a in ((w1_sb[:, pe_, :, :], w1[bass.ds(e, 1), :, :].rearrange("e (k p) f -> p (e k) f", p=P)),
                                   (w2_sb[:, pe_, :, :], w2[bass.ds(e, 1), :, :].rearrange("e (k p) d -> p (e k) d", p=P)),
                                   (b1_sb[:, pe_, :], b1[bass.ds(e, 1), :, :].rearrange("e p k -> p (e k)")),
                                   (b2_sb[:, pe_, :], b2[bass.ds(e, 1), :].to_broadcast([P, D]))):
                        sp.dma_start(dst, a).then_inc(w_in.sems[pe_], 16)
                if t_mm.due(q - 2):
                    sp.wait_ge(t_mm.sem, t_mm.count(q - 2))
                sp.dma_start(rows[:, u, :, :], slots[bass.ds(q * CHUNK, CHUNK), :].rearrange("(c p) d -> p c d", p=P))\
                  .then_inc(rows_in.sems[u], 16)
            turns(sp, load)

        @block.gpsimd
        def _(pool):
            def store(q, e, u, pe_):
                pool.wait_ge(o_ev.sem, o_ev.count(q))
                if sent.due(q - 2):
                    pool.wait_ge(sent.sems[u], sent.count(q - 2, u))
                pool.sem_inc(fence)
                pool.dma_start(results[bass.ds(q * CHUNK, CHUNK), :].rearrange("(c p) d -> p c d", p=P),
                               res[:, u, :, :]).then_inc(sent.sems[u], 16)
            turns(pool, store)
            for u in range(2):
                pool.wait_ge(sent.sems[u], sent.count(CHUNKS - 2 + u, u))
        @block.tensor
        def _(pe):
            pe.wait_ge(id_in, 16)

            def to_columns(q, u):
                pe.wait_ge(rows_in.sems[u], rows_in.count(q, u))
                for c in range(CT):
                    if c >= 2:
                        pe.wait_ge(t_ev.sem, t_ev.count(q, c - 1))
                    elif c == 0:
                        if t_ev.due(q - 1):
                            pe.wait_ge(t_ev.sem, t_ev.count(q - 1))
                    for k in range(KD):
                        mm = nc.tensor.transpose(ps_t[:, c % 2, k * P:(k + 1) * P], rows[:, u, c, k * P:(k + 1) * P],
                                                 ident[:, :])
                    mm.then_inc(t_mm.sem, 1)

            def hidden(q, u, pe_, e):
                if u == 0:
                    pe.wait_ge(w_in.sems[pe_], w_in.count(e, pe_))
                pe.wait_ge(t_ev.sem, t_ev.count(q))
                for m in range(FT):
                    for half in range(2):
                        n = 2 * m + half
                        if n >= 4:
                            pe.wait_ge(h_ev.sem, h_ev.count(q, n - 3))
                        elif n == 0:
                            if h_ev.due(q - 1):
                                pe.wait_ge(h_ev.sem, h_ev.count(q - 1))
                        for k in range(KD):
                            mm = nc.tensor.matmul(ps_h[:, n % 4, 0:HALF], w1_sb[:, pe_, k, m * P:(m + 1) * P],
                                                  cols[:, u, k, half * HALF:(half + 1) * HALF],
                                                  start=(k == 0), stop=(k == KD - 1))
                        mm.then_inc(h_mm.sem, 1)

            def output(q, pe_):
                pe.wait_ge(h_ev.sem, h_ev.count(q))
                for c in range(CT):
                    if c >= 2:
                        pe.wait_ge(o_ev.sem, o_ev.count(q, c - 1))
                    elif c == 0:
                        if o_ev.due(q - 1):
                            pe.wait_ge(o_ev.sem, o_ev.count(q - 1))
                    for k in range(FT):
                        mm = nc.tensor.matmul(ps_o[:, c % 2, 0:D], hid[:, k, c * P:(c + 1) * P], w2_sb[:, pe_, k, :],
                                              start=(k == 0), stop=(k == FT - 1))
                    mm.then_inc(o_mm.sem, 1)

            def emit(q, e, u, pe_):
                hidden(q, u, pe_, e)
                if not isinstance(q, int) or q + 1 < CHUNKS:
                    to_columns(q + 1, 1 - u)
                output(q, pe_)
            to_columns(0, 0)
            turns(pe, emit)

        @block.scalar
        def _(act):
            def emit(q, e, u, pe_):
                if u == 0:
                    act.wait_ge(w_in.sems[pe_], w_in.count(e, pe_))
                for m in range(FT):
                    for half in range(2):
                        act.wait_ge(h_mm.sem, h_mm.count(q, 2 * m + half + 1))
                        if m == half == 0:
                            if o_mm.due(q - 1):
                                act.wait_ge(o_mm.sem, o_mm.count(q - 1))
                        nc.scalar.activation(hid[:, m, half * HALF:(half + 1) * HALF], ps_h[:, (2 * m + half) % 4, 0:HALF],
                                             ACT.Gelu, bias=b1_sb[:, pe_, m:m + 1]).then_inc(h_ev.sem, 1)
            turns(act, emit)

        @block.vector
        def _(dve):
            def columns(q, u):
                for c in range(CT):
                    dve.wait_ge(t_mm.sem, t_mm.count(q, c + 1))
                    if c == 0:
                        if h_mm.due(q - 2):
                            dve.wait_ge(h_mm.sem, h_mm.count(q - 2))
                    nc.vector.tensor_copy(cols[:, u, :, c * P:(c + 1) * P],
                                          ps_t[:, c % 2, 0:D].rearrange("p (k s) -> p k s", k=KD)).then_inc(t_ev.sem, 1)

            def emit(q, e, u, pe_):
                if not isinstance(q, int) or q + 1 < CHUNKS:
                    columns(q + 1, 1 - u)
                if u == 0:
                    dve.wait_ge(w_in.sems[pe_], w_in.count(e, pe_))
                if sent.due(q - 2):
                    dve.wait_ge(sent.sems[u], sent.count(q - 2, u))
                for c in range(CT):
                    dve.wait_ge(o_mm.sem, o_mm.count(q, c + 1))
                    nc.vector.tensor_tensor(res[:, u, c, :], ps_o[:, c % 2, 0:D], b2_sb[:, pe_, :], ALU.add)\
                      .then_inc(o_ev.sem, 1)
            columns(0, 0)
            turns(dve, emit)


def combine(nc, x2_dram, results, slot_g, weight, out):
    with ExitStack() as ctx:
        def sb(name, shape, dt=F32):
            return ctx.enter_context(nc.sbuf_tensor(name, shape, dt))

        def sem(name):
            return ctx.enter_context(nc.semaphore(name))

        index = sb("c_index", [P, 2, TOP, GT], U32)
        w_now = sb("c_weight", [P, 2, TOP, GT])
        rows = sb("c_rows", [P, 2, GT, D])
        got = [sb(f"c_got{c}", [P, 2, GT, D]) for c in range(TOP)]
        stats = sb("c_stats", [P, 2, GT, 6])
        mv = sb("c_mv", [P, 2, GT, 2])
        veps = sb("c_veps", [P, 2, GT])
        rstd = sb("c_rstd", [P, 2, GT])
        minus_half = sb("c_minus_half", [P, GT])
        done = sb("c_done", [P, 2, GT, D])
        come = Turns([sem("c_come0"), sem("c_come1")], 16)
        fetched = Turns([sem("c_got0s"), sem("c_got1s")], 16 * TOP * GT)
        sent = Turns([sem("c_sent0"), sem("c_sent1")], 16)
        staged = Steps(sem("c_staged"), 2)
        summed = Steps(sem("c_summed"), 5 * GT)
        inv = Steps(sem("c_inv"), 2)
        const = sem("c_const")
        fences = [sem("c_fence_pool"), sem("c_fence_dve")]
        block = ctx.enter_context(nc.Block())
        out_rows = out.rearrange("b s d -> (b s) d")

        @block.sync
        def _(sp):
            def load(q, u):
                if summed.due(q - 2, TOP * GT):
                    sp.wait_ge(summed.sem, summed.count(q - 2, TOP * GT))
                sp.dma_start(rows[:, u, :, :], x2_dram[bass.ds(q * (GT * P), GT * P), :]
                             .rearrange("(g p) d -> p g d", p=P)).then_inc(come.sems[u], 16)
            in_pairs(sp, GROUPS, load)

        @block.scalar
        def _(act):
            def store(q, u):
                act.wait_ge(summed.sem, summed.count(q))
                if sent.due(q - 2):
                    act.wait_ge(sent.sems[u], sent.count(q - 2, u))
                act.dma_start(out_rows[bass.ds(q * (GT * P), GT * P), :].rearrange("(g p) d -> p g d", p=P),
                              done[:, u, :, :]).then_inc(sent.sems[u], 16)
            in_pairs(act, GROUPS, store)
            for u in range(2):
                act.wait_ge(sent.sems[u], sent.count(GROUPS - 2 + u, u))

        @block.gpsimd
        def _(pool):
            pool.memset(minus_half[:, :], -0.5).then_inc(const, 1)

            def gather(q, u):
                pool.wait_ge(staged.sem, staged.count(q))
                if summed.due(q - 2, TOP * GT):
                    pool.wait_ge(summed.sem, summed.count(q - 2, TOP * GT))
                pool.sem_inc(fences[0])
                for g in range(GT):
                    for c in range(TOP):
                        nc.gpsimd.indirect_dma_start(
                            out=got[c][:, u, g, :], out_offset=None, in_=results[:, :],
                            in_offset=bass.IndirectOffsetOnAxis(ap=index[:, u, c, g:g + 1], axis=0),
                            bounds_check=ROWS - 1, oob_is_err=False,
                        ).then_inc(fetched.sems[u], 16)

            def inverse_deviation(q, u):
                pool.wait_ge(summed.sem, summed.count(q, 4 * GT))
                pool.wait_ge(const, 1)
                pool.sem_inc(fences[0])
                nc.gpsimd.tensor_scalar(veps[:, u, :], mv[:, u, :, 1], EPS, None, ALU.add).then_inc(inv.sem, 1)
                pool.wait_ge(inv.sem, inv.count(q, 1))
                pool.sem_inc(fences[0])
                nc.gpsimd.tensor_tensor(rstd[:, u, :], veps[:, u, :], minus_half[:, :], ALU.pow).then_inc(inv.sem, 1)

            def emit(q, u):
                if not isinstance(q, int) or q + 1 < GROUPS:
                    gather(q + 1, 1 - u)
                inverse_deviation(q, u)
            gather(0, 0)
            in_pairs(pool, GROUPS, emit)

        @block.vector
        def _(dve):
            def stage(q, u):
                if fetched.due(q - 2):
                    dve.wait_ge(fetched.sems[u], fetched.count(q - 2, u))
                if summed.due(q - 2):
                    dve.wait_ge(summed.sem, summed.count(q - 2))
                nc.vector.tensor_copy(index[:, u, :, :], slot_g[:, :, bass.ds(q * GT, GT)]).then_inc(staged.sem, 1)
                nc.vector.tensor_copy(w_now[:, u, :, :], weight[:, :, bass.ds(q * GT, GT)]).then_inc(staged.sem, 1)

            def emit(q, u):
                if not isinstance(q, int) or q + 1 < GROUPS:
                    stage(q + 1, 1 - u)
                dve.wait_ge(come.sems[u], come.count(q, u))
                dve.wait_ge(fetched.sems[u], fetched.count(q, u))
                dve.wait_ge(staged.sem, staged.count(q))
                for c in range(TOP):
                    if c:
                        dve.wait_ge(summed.sem, summed.count(q, c * GT))
                    for g in range(GT):
                        nc.vector.scalar_tensor_tensor(got[c][:, u, g, :], got[c][:, u, g, :], w_now[:, u, c, g:g + 1],
                                                       (rows if c == 0 else got[0])[:, u, g, :], ALU.mult, ALU.add)\
                          .then_inc(summed.sem, 1)
                dve.wait_ge(summed.sem, summed.count(q, TOP * GT))
                for g in range(GT):
                    nc.vector.bn_stats(stats[:, u, g, :], got[1][:, u, g, :]).then_inc(summed.sem, 1)
                dve.wait_ge(summed.sem, summed.count(q, 3 * GT))
                dve.sem_inc(fences[1])
                for g in range(GT):
                    nc.vector.bn_aggr(mv[:, u, g, :], stats[:, u, g, :]).then_inc(summed.sem, 1)
                dve.wait_ge(inv.sem, inv.count(q))
                if sent.due(q - 2):
                    dve.wait_ge(sent.sems[u], sent.count(q - 2, u))
                for g in range(GT):
                    nc.vector.tensor_scalar(done[:, u, g, :], got[1][:, u, g, :], mv[:, u, g, 0:1], rstd[:, u, g:g + 1],
                                            ALU.subtract, ALU.mult).then_inc(summed.sem, 1)
            stage(0, 0)
            in_pairs(dve, GROUPS, emit)


def rope_tables():
    inverse = (1.0 / 10000.0 ** (np.arange(0, R, 2, dtype=np.float32) / np.float32(R))).astype(np.float32)
    angle = np.outer(np.arange(S, dtype=np.float32), inverse).astype(np.float32)
    return np.cos(angle), np.sin(angle)


def program(nc, a, out):
    NB = 32
    x2_dram = nc.dram_tensor("x2_dram", (NB, S, D), F32).ap()
    slots = nc.dram_tensor("slots_dram", (ROWS, D), F32).ap()
    results = nc.dram_tensor("results_dram", (ROWS, D), F32).ap()
    x2_rows = x2_dram.rearrange("b s d -> (b s) d")
    with ExitStack() as ctx:
        slot_s = ctx.enter_context(nc.sbuf_tensor("slot_s", [P, TOP, TILES], U32))
        slot_g = ctx.enter_context(nc.sbuf_tensor("slot_g", [P, TOP, TILES], U32))
        weight = ctx.enter_context(nc.sbuf_tensor("weight", [P, TOP, TILES], F32))
        logits = ctx.enter_context(nc.sbuf_tensor("logits", [P, NB, T2, E], F32))
        attention(nc, a["x"], a["xT"], a["ctxT"], a["mask"], {"qk": a["s_qk"], "v": a["s_v"]},
                  {"q": a["c_q"], "k": a["c_k"], "v": a["c_v"], "o": a["c_o"]},
                  {"q": a["b_q"], "k": a["b_k"], "v": a["b_v"], "o": a["b_o"]},
                  {"cos": a["cos"], "sin": a["sin"], "ident": a["ident"]},
                  {"w": a["r_w"], "b": a["r_b"]}, x2_dram, slots, logits, NB)
        routing(nc, logits, a, slot_s, slot_g, weight)
        dispatch(nc, x2_rows, slots, slot_s)
        experts(nc, slots, results, a["ident"], a["w1"], a["b1"], a["w2"], a["b2"])
        combine(nc, x2_rows, results, slot_g, weight, out)


def kernel(**inputs):
    from concourse import bacc
    from concourse.bass_utils import run_bass_kernel_spmd

    def array(name):
        return np.asarray(inputs[name])

    def halves(w):
        return w.reshape(H, R // 2, 2, D).transpose(0, 2, 1, 3).reshape(D, D)

    cos, sin = rope_tables()
    arrays = {
        "x": array("x"),
        "xT": array("x").transpose(0, 2, 1),
        "ctxT": array("ctx_1024").transpose(0, 2, 1),
        "mask": array("mask_Bx1x1xS2_ik0").reshape(32, T2, P).transpose(2, 0, 1).reshape(P, 32 * T2),
        "s_qk": np.concatenate([halves(array("L0_attn_wq")), halves(array("L0_attn_wk"))], 0).T,
        "s_v": array("L0_attn_wv").T,
        "c_q": array("L0_xattn_Wq").T,
        "c_k": array("L0_xattn_Wk").T,
        "c_v": array("L0_xattn_Wv").T,
        "c_o": array("L0_xattn_Wo").T,
        "b_q": array("L0_xattn_bq"),
        "b_k": array("L0_xattn_bk"),
        "b_v": array("L0_xattn_bv"),
        "b_o": array("L0_xattn_bo"),
        "r_w": array("L0_ffn_router_w"),
        "r_b": array("L0_ffn_router_b"),
        "w1": array("L0_ffn_w1"),
        "b1": array("L0_ffn_b1").reshape(E, FT, P).transpose(0, 2, 1),
        "w2": array("L0_ffn_w2"),
        "b2": array("L0_ffn_b2"),
        "cos": cos,
        "sin": sin,
        "ident": np.eye(P, dtype=np.float32),
        "upto": np.triu(np.ones((P, P), np.float32)),
        "rank": np.arange(E, 0, -1).astype(np.float32),
        "first_slot": (np.arange(E) * CAP).astype(np.float32),
    }
    nc = bacc.Bacc("TRN2", target_bir_lowering=False, num_devices=1)
    a, given = {}, {}
    for name, value in arrays.items():
        value = np.ascontiguousarray(value)
        given[f"in_{name}"] = value
        a[name] = nc.dram_tensor(f"in_{name}", value.shape, mybir.dt.from_np(value.dtype), kind="ExternalInput").ap()
    out = nc.dram_tensor("out_0", (32, S, D), F32, kind="ExternalOutput").ap()
    program(nc, a, out)
    result = run_bass_kernel_spmd(nc, [given], core_ids=[0])
    return result.results[0]["out_0"]
```
